# Optimizing a Trainium2 kernel written in Bass

```python
import numpy as np
import jax
import jax.numpy as jnp

def _softmax(x, axis=-1):
    return jax.nn.softmax(x, axis=axis)

def _gelu(x):
    return jax.nn.gelu(x, approximate=True)

def _silu(x):
    return jax.nn.silu(x)

def _sigmoid(x):
    return jax.nn.sigmoid(x)

def _layernorm(x, axis=-1, eps=1e-05):
    m = jnp.mean(x, axis=axis, keepdims=True)
    v = jnp.var(x, axis=axis, keepdims=True)
    return (x - m) / jnp.sqrt(v + eps)

def _scatter_add(tgt, idx, src, axis=0):
    return tgt.at[idx].add(src)

def _segment_sum(src, seg, n):
    return jax.ops.segment_sum(src, seg, n)
kernel_name = 'mk_xattn_seq_d1_seqx_r8_ac7d20'

def setup_inputs(seed: int=0):
    np.random.seed(seed)
    _w = jnp.asarray

    def _rec_inputs():
        import jax
        import jax.numpy as jnp
        _rk = jax.random.key(seed)
        x = -0.0002928 + 1 * jax.random.normal(jax.random.fold_in(_rk, 1), (16, 64, 256), jnp.float32)
        _lenS = 64 - jax.random.randint(jax.random.fold_in(_rk, 7), (16,), 0, max(1, 64 // 4) + 1, jnp.int32)
        _lenS2 = 64 - jax.random.randint(jax.random.fold_in(_rk, 8), (16,), 0, max(1, 64 // 4) + 1, jnp.int32)
        _ctx_2048P = jax.random.normal(jax.random.fold_in(_rk, 11), (16, 16, 256), jnp.float32)
        _ctx_2048c = jax.random.dirichlet(jax.random.fold_in(_rk, 511), 0.3 * jnp.ones((16,), jnp.float32), (16, 64))
        _ctx_2048t = jnp.einsum('bsk,bkd->bsd', _ctx_2048c, _ctx_2048P)
        _ctx_2048t = _ctx_2048t * jax.lax.rsqrt(jnp.mean(jnp.square(_ctx_2048t)) + 1e-12) * 0.953939
        ctx_2048 = -1.39393e-06 + 0.999914 * (_ctx_2048t + 0.3 * jax.random.normal(jax.random.fold_in(_rk, 611), (16, 64, 256), jnp.float32))
        return (x, ctx_2048)
    x, ctx_2048 = _rec_inputs()

    def _L0_xattn_setup():
        import jax, jax.numpy as jnp
        import numpy as np
        N, C, S, S2, H, CTX = (4, 64, 256, 256, 8, 64)
        EPS = 1e-05
        key = jax.random.key(seed)
        ks = jax.random.split(key, 6)
        sd = lambda fan: 1.0 / np.sqrt(fan)
        return {'input': jax.random.normal(ks[0], (N, C, S), jnp.float32), 'context': jax.random.normal(ks[1], (N, CTX, S2), jnp.float32), 'gamma': jnp.ones((C,), jnp.float32), 'beta': jnp.zeros((C,), jnp.float32), 'Wq': jax.random.normal(ks[2], (C * H, C), jnp.float32) * sd(C), 'bq': jnp.zeros((C * H,), jnp.float32), 'Wkv': jax.random.normal(ks[3], (C * H * 2, CTX), jnp.float32) * sd(CTX), 'bkv': jnp.zeros((C * H * 2,), jnp.float32), 'Wo': jax.random.normal(ks[4], (C, C * H), jnp.float32) * sd(C * H), 'bo': jnp.zeros((C,), jnp.float32)}
    _L0_xattn_all = _L0_xattn_setup()
    _L0_xattn_in = {k: v for k, v in _L0_xattn_all.items() if k in ('gamma', 'beta', 'Wq', 'bq', 'Wkv', 'bkv', 'Wo', 'bo')}
    del _L0_xattn_all
    return {'x': x, 'ctx_2048': ctx_2048, 'L0_xattn_gamma': _L0_xattn_in['gamma'], 'L0_xattn_beta': _L0_xattn_in['beta'], 'L0_xattn_Wq': _L0_xattn_in['Wq'], 'L0_xattn_bq': _L0_xattn_in['bq'], 'L0_xattn_Wkv': _L0_xattn_in['Wkv'], 'L0_xattn_bkv': _L0_xattn_in['bkv'], 'L0_xattn_Wo': _L0_xattn_in['Wo'], 'L0_xattn_bo': _L0_xattn_in['bo']}

def reference(x, ctx_2048, L0_xattn_gamma, L0_xattn_beta, L0_xattn_Wq, L0_xattn_bq, L0_xattn_Wkv, L0_xattn_bkv, L0_xattn_Wo, L0_xattn_bo):
    import jax
    import jax.numpy as jnp

    def _L0_xattn_ref(input, context, gamma, beta, Wq, bq, Wkv, bkv, Wo, bo):
        import jax, jax.numpy as jnp
        import numpy as np
        N, C, S, S2, H, CTX = (4, 64, 256, 256, 8, 64)
        EPS = 1e-05
        n, c, s = input.shape
        h = H
        mu = jnp.mean(input, axis=(1, 2), keepdims=True)
        var = jnp.var(input, axis=(1, 2), keepdims=True)
        xn = (input - mu) * jax.lax.rsqrt(var + EPS)
        xn = xn * gamma[None, :, None] + beta[None, :, None]
        q = jnp.einsum('oc,ncs->nos', Wq, xn) + bq[None, :, None]
        kv = jnp.einsum('od,nds->nos', Wkv, context) + bkv[None, :, None]
        q = q.reshape(n, h, c, s).transpose(0, 1, 3, 2)
        kv = kv.reshape(n, 2 * h, c, -1).transpose(0, 1, 3, 2)
        k, v = (kv[:, :h], kv[:, h:])
        scale = c ** (-0.25)
        att = jax.nn.softmax(jnp.einsum('nhqc,nhkc->nhqk', q * scale, k * scale), axis=-1)
        y = jnp.einsum('nhqk,nhkc->nhqc', att, v)
        y = y.transpose(0, 1, 3, 2).reshape(n, h * c, s)
        out = jnp.einsum('co,nos->ncs', Wo, y) + bo[None, :, None]
        return input + out
    x = _L0_xattn_ref(x, ctx_2048, L0_xattn_gamma, L0_xattn_beta, L0_xattn_Wq, L0_xattn_bq, L0_xattn_Wkv, L0_xattn_bkv, L0_xattn_Wo, L0_xattn_bo)
    return x

_drawn_inputs = setup_inputs


def setup_inputs(seed=0):
    import zlib

    import numpy as np

    out = dict(_drawn_inputs(seed))
    spreads = {'L0_xattn_gamma': (1.0, 0.2),
     'L0_xattn_beta': (0.0, 0.1),
     'L0_xattn_bq': (0.0, 0.1),
     'L0_xattn_bkv': (0.0, 0.1),
     'L0_xattn_bo': (0.0, 0.1)}
    factors = {}
    for name, (base, spread) in spreads.items():
        noise = np.random.default_rng([zlib.crc32(name.encode()), seed]).standard_normal(out[name].shape)
        drawn = base * np.exp(spread * noise) if base else spread * noise
        out[name] = jnp.asarray(drawn.astype(out[name].dtype))
    for name, factor in factors.items():
        out[name] = (out[name] * factor).astype(out[name].dtype)
    return out
```

```python
import concourse.bass as bass
import concourse.mybir as mybir
from concourse.alu_op_type import AluOpType as ALU
from contextlib import ExitStack

N, C, S, H = 16, 64, 256, 8
P = 128
KT = S // P
PAIRS = H // 2
EPS = 1e-5
DIRECT = 2
T_EARLY = 6
T_AHEAD, MAX_AHEAD, AV_BEHIND = 14, 12, 3
CHUNK = 4
GROUPS = ((0, CHUNK), (CHUNK, N))
U_TOP = 16384.0
U_W = C + 2
W_V, W_O, W_BQ = 0, H * C, 2 * H * C
W_BV = W_BQ + H
W_BO = W_BV + H
W_GAMMA, W_BETA = W_BO + 1, W_BO + 2
W_COLS = W_BETA + 1


def xattn_program(nc, x_in, ctx_in, ctx_flat_in, wq_in, wk_in, w_in, out):
    fp32, fp32r, fp16 = mybir.dt.float32, mybir.dt.float32r, mybir.dt.float16
    ACT = mybir.ActivationFunctionType
    X = mybir.AxisListType.X
    stack = ExitStack()
    with stack:
        def sb(name, shape, dt):
            return stack.enter_context(nc.sbuf_tensor(name, shape, dt))

        def ps(name, shape):
            return stack.enter_context(nc.psum_tensor(name, shape, fp32))

        def sem(name):
            return stack.enter_context(nc.semaphore(name))

        x_raw = sb("x_raw", [P, N, S], fp32)
        ctx_raw = sb("ctx_raw", [P, 2, CHUNK, S], fp32)
        w_sb = sb("w_sb", [P, W_COLS], fp32)
        wq2 = sb("wq2", [C, H, 2, C], fp32)
        wk2 = sb("wk2", [C, H, 2, C], fp32)
        xn = sb("xn", [P, 2, CHUNK, S], fp32)
        x_all = sb("x_all", [P, N, 2, S], fp32r)
        c_all = sb("c_all", [P, N, 2, S], fp32r)
        a_hi = sb("a_hi", [P, H, 2 * C], fp32r)
        a_lo = sb("a_lo", [P, H, 2 * C], fp32r)
        b_sb = sb("b_sb", [P, H * C], fp32)
        b_w = sb("b_w", [P, H * C], fp32r)
        bo2 = sb("bo2", [P, 1], fp32)
        x_res = sb("x_res", [P, N, P], fp32)
        x_seq = sb("x_seq", [P, 2, 2, S], fp32r)
        c_max = sb("c_max", [P, 2, S], fp32r)
        c_seq = sb("c_seq", [P, 2, 2, S], fp32r)
        u_hi = sb("u_hi", [P, 2, KT, H, U_W], fp16)
        u_lo = sb("u_lo", [P, 2, KT, H, C], fp16)
        t_a = sb("t_a", [P, 2, H, S], fp32r)
        t_b = sb("t_b", [P, 2, H, S], fp32r)
        neg_max = sb("neg_max", [P, 2, H, KT], fp32)
        neg_max_rows = sb("neg_max_rows", [H * KT, 2, P], fp32r)
        p_full = sb("p_full", [P, 2, KT * S], fp32)
        p_hi = sb("p_hi", [P, 4, KT, S], fp16)
        p_lo = sb("p_lo", [P, 4, KT, S], fp16)
        inv_sum = sb("inv_sum", [P, 2, 4], fp32)
        z_n = sb("z_n", [P, 2, KT, H * C], fp32)
        ctx_spread = z_n[:].rearrange("p q t k -> p (q t k)")
        z_4 = sb("z_4", [P, KT, 4 * C], fp32)
        z_2 = sb("z_2", [P, KT, 2 * C], fp32)
        z_1 = sb("z_1", [P, KT, C], fp32)
        ident = sb("ident", [P, P], fp32)
        mean_w = sb("mean_w", [P, P], fp32)
        ones_row = sb("ones_row", [1, P], fp32)
        stats = sb("stats", [P, N, 6], fp32)
        dev = sb("dev", [P, N, 2], fp32)
        dev2 = sb("dev2", [P, N, 2], fp32)
        mu = sb("mu", [P, N], fp32)
        var = sb("var", [P, N], fp32)
        root = sb("root", [P, N], fp32)
        y0 = sb("y0", [P, N], fp32)
        y1 = sb("y1", [P, N], fp32)
        y2 = sb("y2", [P, N], fp32)
        rstd = sb("rstd", [P, N], fp32)
        xn_scale = sb("xn_scale", [P, N], fp32)
        xn_shift = sb("xn_shift", [P, N], fp32)
        tops = sb("tops", [P, 2], fp32)
        top = sb("top", [1, 2], fp32)
        u_bound = sb("u_bound", [1, 1], fp32)
        u_unscale = sb("u_unscale", [P, 1], fp32)
        u_scale = sb("u_scale", [P, 1], fp32)

        ps_max = ps("ps_max", [P, 2, KT * S])
        ps_sc = ps("ps_sc", [P, 2, KT * S])
        ps_z = ps("ps_z", [P, 2, 512])
        ps_t = ps("ps_t", [P, 2 * S])
        ps_m = ps("ps_m", [P, 512])
        Z_W = C + 1

        dma_x = [sem(f"dma_x{g}") for g in range(len(GROUPS))]
        dma_w, dma_flat = sem("dma_w"), sem("dma_flat")
        dma_c = [sem(f"dma_c{c}") for c in range(N // CHUNK)]
        pool_const, pool_ones = sem("pool_const"), sem("pool_ones")
        pool_c_hi, pool_c_lo, pool_xb = sem("pool_c_hi"), sem("pool_c_lo"), sem("pool_xb")
        dve_step = sem("dve_step")
        dve_stats, dve_q, dve_var, dve_xn, dve_xlo = sem("dve_stats"), sem("dve_q"), sem("dve_var"), sem("dve_xn"), sem("dve_xlo")
        dve_tops, dve_bound, dve_scale, dve_bw, dve_alo = sem("dve_tops"), sem("dve_bound"), sem("dve_scale"), sem("dve_bw"), sem("dve_alo")
        act_root, act_ahi, act_xhi, act_b = sem("act_root"), sem("act_ahi"), sem("act_xhi"), sem("act_b")
        pe_mean, pe_var, pe_a, pe_bw, pe_tops, pe_bound = sem("pe_mean"), sem("pe_var"), sem("pe_a"), sem("pe_bw"), sem("pe_tops"), sem("pe_bound")
        dma_xseq = [sem(f"dma_xseq{b}") for b in range(2)]
        dma_cmax = [sem(f"dma_cmax{b}") for b in range(2)]
        dma_cseq = [sem(f"dma_cseq{b}") for b in range(2)]
        dma_tb = [[sem(f"dma_tb{b}{p}") for p in range(PAIRS)] for b in range(2)]
        dma_negmax = [sem(f"dma_negmax{b}") for b in range(2)]
        dma_out = [sem(f"dma_out{b}") for b in range(2)]
        pe_t, pe_s1, pe_s2, pe_av = sem("pe_t"), sem("pe_s1"), sem("pe_s2"), sem("pe_av")
        pe_u, pe_mt, pe_y = sem("pe_u"), sem("pe_mt"), sem("pe_y")
        act_thi, act_phi, act_p = sem("act_thi"), sem("act_phi"), sem("act_p")
        dve_tlo, dve_max, dve_inv, dve_zn = sem("dve_tlo"), sem("dve_max"), sem("dve_inv"), sem("dve_zn")
        dve_ulo, dve_y = sem("dve_ulo"), sem("dve_y")
        act_uhi, act_mt = sem("act_uhi"), sem("act_mt")
        pool_plo, pool_z4, pool_z2, pool_z1 = sem("pool_plo"), sem("pool_z4"), sem("pool_z2"), sem("pool_z1")

        block = stack.enter_context(nc.Block())

        def need(eng, s, count):
            if not (isinstance(count, int) and count <= 0):
                eng.wait_ge(s, count)

        def at(n, h, shift):
            dn, head = divmod(h + shift, H)
            seq = n + dn
            if isinstance(seq, int) and not 0 <= seq < N:
                return None
            return seq, dn, head

        def peeled_step(n, h, at_n, at_h):
            return isinstance(n, int) and (n, h) == (at_n, at_h)

        def direct(m):
            return isinstance(m, int) and m < DIRECT

        def chunks_by(n, m):
            return N // CHUNK if n == FIRST - 1 else m // CHUNK + 1

        def t_banks(turn):
            return 3 if isinstance(turn, int) and turn < T_EARLY else 1

        def t_bank(turn):
            return (ps_t[:], ps_z[:, 0], ps_z[:, 1])[turn % 3 if t_banks(turn) == 3 else 0]

        FIRST, LAST = 2, 11

        def run(eng, step):
            for n in range(-3, FIRST):
                for h in range(H):
                    step(n, n // 2, n % 2, h)
            with eng.Fori(FIRST // 2, (LAST + 1) // 2) as pair:
                for par in range(2):
                    for h in range(H):
                        step(pair * 2 + par, pair, par, h)
            for n in range(LAST + 1, N + 2):
                for h in range(H):
                    step(n, n // 2, n % 2, h)

        def fills(half, par, dn):
            return half + (par + dn) // 2 + 1

        def load_ctx(eng, c):
            for part in range(2):
                eng.dma_start(ctx_raw[part * C:(part + 1) * C, c % 2], ctx_in[:, c * CHUNK:(c + 1) * CHUNK, :]).then_inc(dma_c[c], 16)

        @block.sync
        def _(sp):
            for g, (first, end) in enumerate(GROUPS):
                for part in range(2):
                    sp.dma_start(x_raw[part * C:(part + 1) * C, first:end], x_in[:, first:end, :]).then_inc(dma_x[g], 16)
                if g == 0:
                    load_ctx(sp, 0)
            sp.dma_start(ctx_spread, ctx_flat_in).then_inc(dma_flat, 16)
            for c in range(1, N // CHUNK):
                need(sp, pool_c_lo, c - 1)
                load_ctx(sp, c)
            x_from, x_to, c_from = x_all[:].bitcast(fp32), x_seq[:].bitcast(fp32), c_all[:].bitcast(fp32)
            c_to, c_max_to, rows_from = c_seq[:].bitcast(fp32), c_max[:].bitcast(fp32), neg_max_rows[:].bitcast(fp32)
            t_a_from, t_b_to = t_a[:].bitcast(fp32), t_b[:].bitcast(fp32)

            def step(n, half, par, h):
                if h == 3 and (e := at(n, 0, -2 * H)):
                    m, dn, _ = e
                    need(sp, dve_y, m + 1)
                    sp.dma_start(out[:, bass.ds(m, 1), :], x_res[:, bass.ds(m, 1), :]).then_inc(dma_out[par], 16)
                if h == 1 and (e := at(n, 0, H)):
                    m, dn, _ = e
                    q = (par + dn) % 2
                    need(sp, pe_s2, (n - 1) * H + H)
                    if isinstance(n, int):
                        need(sp, pool_const, 7)
                    if isinstance(n, int):
                        need(sp, pool_c_lo, chunks_by(n, m))
                    sp.dma_start(c_to[:, q, :, :], c_from[:, bass.ds(m, 1), :, :].rearrange("p o a s -> p (o a) s")).then_inc(dma_cseq[q], 16)
                if h == 5 and (e := at(n, 0, 3 * H)) and not direct(e[0]):
                    m, dn, _ = e
                    q = (par + dn) % 2
                    need(sp, pe_t, (n + 1) * PAIRS + PAIRS)
                    need(sp, pe_s1, (n + 1) * H + H)
                    if isinstance(n, int):
                        need(sp, act_xhi, 2 * chunks_by(n, m))
                        need(sp, dve_xlo, chunks_by(n, m))
                        need(sp, pool_ones, chunks_by(n, m))
                        need(sp, pool_c_hi, chunks_by(n, m))
                    sp.dma_start(x_to[:, q, :, :], x_from[:, bass.ds(m, 1), :, :].rearrange("p o a s -> p (o a) s")).then_inc(dma_xseq[q], 16)
                    sp.dma_start(c_max_to[:, q:q + 1, :], c_from[:, bass.ds(m, 1), 0, :]).then_inc(dma_cmax[q], 16)
                if h % 2 == 1 and (e := at(n, h - 1, T_AHEAD)):
                    m, dn, head = e
                    q = (par + dn) % 2
                    need(sp, act_thi, m * PAIRS + head // 2 + 1)
                    sp.dma_start(t_b_to[0:C, q, head:head + 2, :], t_a_from[0:C, q, head:head + 2, :]).then_inc(dma_tb[q][head // 2], 16)
                if h == 6 and (e := at(n, 0, H)):
                    m, dn, _ = e
                    q = (par + dn) % 2
                    need(sp, pe_s2, n * H)
                    need(sp, act_mt, m + 1)
                    sp.dma_start(t_b_to[C:C + 1, q, :, :].rearrange("o h (t s) -> o (h t) s", t=KT),
                                 rows_from[:, q, :]).then_inc(dma_negmax[q], 16)

            run(sp, step)
            for b in range(2):
                sp.wait_ge(dma_out[b], 16 * (N // 2))

        @block.tensor
        def _(pe):
            mm = nc.tensor.matmul
            pe.wait_ge(dma_w, 16 * 6)
            for h in range(H):
                cols = slice(h * 2 * C % (KT * S), h * 2 * C % (KT * S) + 2 * C)
                bank = h * 2 * C // (KT * S)
                wk_h = wk2[:, h, :, :].rearrange("o d c -> o (d c)")
                mm(ps_max[:, bank, cols], wq2[:, h, :, :].rearrange("o d c -> o (d c)"), wk_h, start=True, stop=True)
                mm(ps_sc[C:C + 1, bank, cols], w_sb[0:C, W_BQ + h:W_BQ + h + 1], wk_h, start=True, stop=True)
                last = mm(ps_sc[C + 32:C + 33, bank, cols], w_sb[0:C, W_BQ + h:W_BQ + h + 1], wk_h, start=True, stop=True)
            last.then_inc(pe_a, 1)
            for h in range(H):
                wo_h = w_sb[0:C, W_O + h * C:W_O + (h + 1) * C]
                mm(ps_z[0:C, 0, h * C:(h + 1) * C], w_sb[0:C, W_V + h * C:W_V + (h + 1) * C], wo_h, start=True, stop=True)
                for half in range(2):
                    last = mm(ps_z[half * C:(half + 1) * C, 1, 0:1], wo_h, w_sb[0:C, W_BV + h:W_BV + h + 1], start=(h == 0),
                              stop=(h == H - 1))
            last.then_inc(pe_bw, 1)
            pe.wait_ge(pool_const, 4)

            def statistics(g, first, end):
                k = end - first
                pe.wait_ge(dve_stats, end)
                for a in range(2):
                    last = mm(ps_m[:, a * k:(a + 1) * k], mean_w[:], stats[:, first:end, 1 + 3 * a], start=True, stop=True)
                last.then_inc(pe_mean, 1)
                pe.wait_ge(dve_q, g + 1)
                mm(ps_m[:, 64:64 + 2 * k], mean_w[:], dev2[:, first:end, :].rearrange("p n a -> p (n a)"), start=True,
                   stop=True).then_inc(pe_var, 1)

            def u_bound_everywhere():
                pe.wait_ge(dve_tops, 2)
                nc.tensor.transpose(ps_m[0:1, 0:P], tops[:, 0:1], ident[:])
                nc.tensor.transpose(ps_m[0:1, P:2 * P], tops[:, 1:2], ident[:]).then_inc(pe_tops, 1)
                pe.wait_ge(dve_bound, 1)
                mm(ps_m[:, S:S + 1], ones_row[:], u_bound[:], start=True, stop=True).then_inc(pe_bound, 1)

            statistics(0, *GROUPS[0])
            def step(n, half, par, h):
                if peeled_step(n, h, -1, 0):
                    statistics(1, *GROUPS[1])
                if peeled_step(n, h, -1, 3):
                    u_bound_everywhere()
                if h % 2 == 0 and (e := at(n, h, T_AHEAD)):
                    m, dn, head = e
                    q, turn = (par + dn) % 2, m * PAIRS + head // 2
                    if direct(m):
                        x_m = x_all[:, m]
                        if head == 0:
                            need(pe, act_xhi, 2)
                            need(pe, dve_xlo, 1)
                            need(pe, pool_ones, 1)
                            need(pe, dve_alo, 2)
                    else:
                        x_m = x_seq[:, q]
                        if head == 0:
                            need(pe, dma_xseq[q], 16 * (fills(half, par, dn) - 1))
                    need(pe, dve_tlo, turn - t_banks(turn) + 1)
                    if isinstance(turn, int) and turn == 1:
                        need(pe, act_b, 1)
                        need(pe, dve_bw, 1)
                    bank = t_bank(turn)
                    for k in range(2):
                        mm(bank[:, k * S:(k + 1) * S], a_hi[:, head + k, :], x_m[:, 0, :], start=True, stop=False)
                        last = mm(bank[:, k * S:(k + 1) * S], a_lo[:, head + k, :], x_m[:, 1, :], start=False, stop=True)
                    last.then_inc(pe_t, 1)
                if e := at(n, h, MAX_AHEAD):
                    m, dn, head = e
                    q, bank = (par + dn) % 2, head % 2
                    if direct(m):
                        c_m = c_all[:, m, 0, :]
                        need(pe, pool_c_hi, 1)
                    else:
                        c_m = c_max[:, q, :]
                        if head == 0:
                            need(pe, dma_cmax[q], 16 * (fills(half, par, dn) - 1))
                    if head % 2 == 0:
                        need(pe, dve_tlo, m * PAIRS + head // 2 + 1)
                    need(pe, dve_max, m * H + head - 1)
                    for qt in range(KT):
                        last = mm(ps_max[:, bank, qt * S:(qt + 1) * S], t_a[:, q, head, qt * P:(qt + 1) * P], c_m,
                                  start=True, stop=True)
                    last.then_inc(pe_s1, 1)
                if e := at(n, h, 0):
                    m, dn, head = e
                    bank = head % 2
                    if head == 0:
                        need(pe, dma_cseq[par], 16 * fills(half, par, 0))
                        need(pe, dma_negmax[par], 16 * fills(half, par, 0))
                    if head % 2 == 0:
                        need(pe, dma_tb[par][head // 2], 16 * fills(half, par, 0))
                    need(pe, act_p, m * H + head - 1)
                    for kt in range(KT):
                        keys = slice(kt * P, (kt + 1) * P)
                        mm(ps_sc[:, bank, kt * S:(kt + 1) * S], c_seq[:, par, 0, keys], t_a[:, par, head, :], start=True, stop=False)
                        last = mm(ps_sc[:, bank, kt * S:(kt + 1) * S], c_seq[0:C + 1, par, 1, keys], t_b[0:C + 1, par, head, :],
                                  start=False, stop=True)
                    last.then_inc(pe_s2, 1)
                if e := at(n, h, -AV_BEHIND):
                    m, dn, head = e
                    q, bank, buf = (par + dn) % 2, head // 2 % 2, head % 4
                    if head == 0:
                        need(pe, dve_ulo, 2 * (m + 1))
                    if head % 2 == 0:
                        need(pe, dve_zn, m * PAIRS + head // 2 - 1)
                    need(pe, pool_plo, m * H + head + 1)
                    for qt in range(KT):
                        qs = slice(qt * P, (qt + 1) * P)
                        z0 = (qt * 2 + head % 2) * Z_W
                        for kt in range(KT):
                            u_h, u_l = u_hi[:, q, kt, head, 0:Z_W], u_lo[:, q, kt, head, :]
                            mm(ps_z[:, bank, z0:z0 + Z_W], p_hi[:, buf, kt, qs], u_h, start=(kt == 0), stop=False)
                            mm(ps_z[:, bank, z0:z0 + C], p_hi[:, buf, kt, qs], u_l, start=False, stop=False)
                            last = mm(ps_z[:, bank, z0:z0 + Z_W], p_lo[:, buf, kt, qs], u_h, start=False, stop=(kt == KT - 1))
                    last.then_inc(pe_av, 1)
                if h == 1 and (e := at(n, 0, -2 * H)):
                    m, dn, _ = e
                    need(pe, pool_z1, m + 1)
                    if at(n, 0, 0):
                        need(pe, dve_ulo, 2 * (n + 1))
                    nc.tensor.transpose(ps_m[:, 0:P], z_1[:].rearrange("p t c -> p (t c)"), ident[:]).then_inc(pe_y, 1)
                if h in (3, 7) and (e := at(n, 0, H)):
                    m, dn, _ = e
                    q, kt = (par + dn) % 2, h // 4
                    keys = slice(kt * P, (kt + 1) * P)
                    if kt == 0:
                        need(pe, dma_cseq[q], 16 * fills(half, par, dn))
                        if isinstance(m, int) and m == 0:
                            need(pe, dve_bw, 2)
                        need(pe, dve_y, n - 1)
                    else:
                        need(pe, act_mt, n + 2)
                    mm(ps_m[:], c_seq[:, q, 0, keys], b_w[:], start=True, stop=False)
                    mm(ps_m[:], c_seq[0:C, q, 1, keys], b_w[0:C, :], start=False, stop=True).then_inc(pe_u, 1)
                if h == 5 and (e := at(n, 0, H)):
                    m, dn, _ = e
                    need(pe, dve_max, (m + 1) * H)
                    need(pe, dve_ulo, 2 * m + 1)
                    nc.tensor.transpose(ps_m[0:H * KT, 0:P], neg_max[:, (par + dn) % 2, :, :].rearrange("p h t -> p (h t)"),
                                        ident[:]).then_inc(pe_mt, 1)
            run(pe, step)

        @block.scalar
        def _(act):
            act.dma_start(w_sb[C:P, W_BO:W_COLS], w_in[:, W_BO:W_COLS]).then_inc(dma_w, 16)
            for dup in range(2):
                act.dma_start(wq2[:, :, dup, :], wq_in).then_inc(dma_w, 16)
                act.dma_start(wk2[:, :, dup, :], wk_in).then_inc(dma_w, 16)
            act.dma_start(w_sb[0:C, :], w_in).then_inc(dma_w, 16)
            act.wait_ge(pe_a, 1)
            nc.scalar.activation(a_hi[:].rearrange("p h c -> p (h c)"), ps_max[:].rearrange("p b s -> p (b s)"), ACT.Copy,
                                 scale=C ** -0.5).then_inc(act_ahi, 1)
            act.wait_ge(pool_const, 5)
            nc.scalar.activation(a_lo[C:C + 1].rearrange("p h c -> p (h c)"), ps_sc[C:C + 1].rearrange("p b s -> p (b s)"), ACT.Copy,
                                 scale=C ** -0.5).then_inc(act_ahi, 1)

            def roots(g, first, end):
                act.wait_ge(dve_var, g + 1)
                nc.scalar.activation(root[:, first:end], var[:, first:end], ACT.Sqrt).then_inc(act_root, 1)

            def x_high(c):
                seqs = slice(c * CHUNK, (c + 1) * CHUNK)
                act.wait_ge(dve_xn, (c + 1) * CHUNK)
                nc.scalar.activation(x_all[:, seqs, 1, :], xn[:, c % 2, :, :], ACT.Copy).then_inc(act_xhi, 1)
                nc.scalar.activation(x_all[0:C, seqs, 0, :], xn[0:C, c % 2, :, :], ACT.Copy).then_inc(act_xhi, 1)

            roots(0, *GROUPS[0])
            x_high(0)
            act.wait_ge(pe_bw, 1)
            nc.scalar.activation(b_sb[0:C, :], ps_z[0:C, 0, :], ACT.Copy).then_inc(act_b, 1)

            def step(n, half, par, h):
                if peeled_step(n, h, -1, 0):
                    roots(1, *GROUPS[1])
                if isinstance(n, int) and n == -1 and h in (1, 3, 5):
                    x_high((h + 1) // 2)
                if h % 2 == 0 and (e := at(n, h, T_AHEAD)):
                    m, dn, head = e
                    need(act, pe_t, m * PAIRS + head // 2 + 1)
                    need(act, pe_s2, (m - 2) * H + head + 2)
                    nc.scalar.activation(t_a[0:C, (par + dn) % 2, head:head + 2, :].rearrange("p h s -> p (h s)"),
                                         t_bank(m * PAIRS + head // 2)[0:C, :], ACT.Copy).then_inc(act_thi, 1)
                if e := at(n, h, 0):
                    m, dn, head = e
                    buf = head % 4
                    scores = ps_sc[:, head % 2, :]
                    need(act, pe_s2, m * H + head + 1)
                    need(act, pe_av, m * H + head - 3)
                    nc.scalar.activation(p_hi[:, buf, :, :].rearrange("p t s -> p (t s)"), scores, ACT.Exp).then_inc(act_phi, 1)
                    need(act, pool_plo, m * H + head - 1)
                    nc.scalar.activation(p_full[:, head % 2, :], scores, ACT.Exp).then_inc(act_p, 1)
                if h in (3, 7) and (e := at(n, 0, H)):
                    m, dn, _ = e
                    q, kt = (par + dn) % 2, h // 4
                    need(act, pe_u, 2 * m + kt + 1)
                    need(act, pe_av, (n - 1) * H + H)
                    if isinstance(m, int):
                        need(act, pool_const, 6)
                    nc.scalar.activation(u_hi[:, q, kt, :, 0:C], ps_m[:].rearrange("p (h c) -> p h c", h=H), ACT.Copy).then_inc(act_uhi, 1)
                if h == 5 and (e := at(n, 0, H)):
                    m, dn, _ = e
                    q = (par + dn) % 2
                    need(act, pe_mt, m + 1)
                    need(act, dma_negmax[q], 16 * (fills(half, par, dn) - 1))
                    nc.scalar.activation(neg_max_rows[:, q, :], ps_m[0:H * KT, 0:P], ACT.Copy).then_inc(act_mt, 1)

            run(act, step)

        @block.gpsimd
        def _(pool):
            nc.gpsimd.memset(ident[:], 0.0).then_inc(pool_const, 1)
            nc.gpsimd.memset(mean_w[:], 1.0 / (2 * P)).then_inc(pool_const, 1)
            nc.gpsimd.memset(ones_row[:], 1.0).then_inc(pool_const, 1)
            pool.wait_ge(pool_const, 3)
            nc.gpsimd.affine_select(out=ident[:], in_=ident[:], compare_op=ALU.not_equal, fill=1.0, base=0,
                                    pattern=[[-1, P]], channel_multiplier=1).then_inc(pool_const, 1)
            pool.wait_ge(pool_const, 4)
            nc.gpsimd.memset(a_lo[C:P].bitcast(fp32), 0.0).then_inc(pool_const, 1)
            pool.wait_ge(pool_const, 5)
            nc.gpsimd.memset(u_hi[:, :, :, :, C:U_W], 1.0).then_inc(pool_const, 1)
            pool.wait_ge(pool_const, 6)

            def split_ctx(c):
                seqs = slice(c * CHUNK, (c + 1) * CHUNK)
                pool.wait_ge(dma_c[c], 32)
                nc.gpsimd.tensor_scalar(c_all[:, seqs, 0, :], ctx_raw[:, c % 2, :, :], 1.0, 1.0, ALU.mult, ALU.mult).then_inc(pool_c_hi, 1)
                pool.wait_ge(pool_c_hi, c + 1)
                nc.gpsimd.tensor_tensor(c_all[0:C, seqs, 1, :], ctx_raw[0:C, c % 2, :, :], c_all[0:C, seqs, 0, :].bitcast(fp32),
                                        ALU.subtract).then_inc(pool_c_lo, 1)
                pool.wait_ge(pool_c_lo, c + 1)

            def ones_under_x(c):
                pool.wait_ge(dve_xlo, c + 1)
                nc.gpsimd.memset(x_all[C:P, c * CHUNK:(c + 1) * CHUNK, 1, :].bitcast(fp32), 1.0).then_inc(pool_ones, 1)
                pool.wait_ge(pool_ones, c + 1)

            split_ctx(0)
            ones_under_x(0)
            nc.gpsimd.memset(c_all[C:P, :, 1, :].bitcast(fp32), 1.0).then_inc(pool_const, 1)
            pool.wait_ge(pool_const, 7)
            for c in range(1, N // CHUNK):
                split_ctx(c)
                ones_under_x(c)
            pool.wait_ge(dve_bw, 1)
            for c in range(N // CHUNK):
                seqs = slice(c * CHUNK, (c + 1) * CHUNK)
                pool.wait_ge(dve_xn, (c + 1) * CHUNK)
                for qt in range(KT):
                    rows = slice(qt * C, (qt + 1) * C)
                    nc.gpsimd.tensor_scalar(x_res[rows, seqs, :], x_raw[rows, seqs, qt * P:(qt + 1) * P], 1.0, bo2[rows], ALU.mult,
                                            ALU.add).then_inc(pool_xb, 1)
                    pool.wait_ge(pool_xb, KT * c + qt + 1)

            def step(n, half, par, h):
                if e := at(n, h, 0):
                    m, dn, head = e
                    buf = head % 4
                    need(pool, act_p, m * H + head + 1)
                    need(pool, pe_av, m * H + head - 3)
                    nc.gpsimd.tensor_tensor(p_lo[:, buf, :, :].rearrange("p t s -> p (t s)"), p_full[:, head % 2, :],
                                            p_hi[:, buf, :, :].rearrange("p t s -> p (t s)"), ALU.subtract).then_inc(pool_plo, 1)
                if h == 3 and (e := at(n, 0, -H)):
                    m, dn, _ = e
                    z = z_n[:, (par + dn) % 2, :, :]
                    need(pool, dve_zn, (m + 1) * PAIRS)
                    nc.gpsimd.tensor_tensor(z_4[:], z[:, :, 0:4 * C], z[:, :, 4 * C:8 * C], ALU.add).then_inc(pool_z4, 1)
                    need(pool, pool_z4, m + 1)
                    nc.gpsimd.tensor_tensor(z_2[:], z_4[:, :, 0:2 * C], z_4[:, :, 2 * C:4 * C], ALU.add).then_inc(pool_z2, 1)
                    need(pool, pool_z2, m + 1)
                    need(pool, pe_y, m)
                    nc.gpsimd.tensor_tensor(z_1[:], z_2[:, :, 0:C], z_2[:, :, C:2 * C], ALU.add).then_inc(pool_z1, 1)

            run(pool, step)

        @block.vector
        def _(dve):
            steps = [0]

            def chain(instruction):
                steps[0] += 1
                instruction.then_inc(dve_step, 1)
                dve.wait_ge(dve_step, steps[0])

            def statistics(g, first, end):
                k = end - first
                seqs = slice(first, end)
                dve.wait_ge(dma_x[g], 32)
                for n in range(first, end):
                    nc.vector.bn_stats(stats[:, n, :], x_raw[:, n, :]).then_inc(dve_stats, 1)
                dve.wait_ge(pe_mean, g + 1)
                chain(nc.vector.tensor_reduce(mu[:, seqs], ps_m[:, 0:2 * k].rearrange("p (a n) -> p n a", a=2), X, ALU.add))
                mu2 = mu[:, seqs].rearrange("p (n a) -> p n a", a=1).broadcast_to([P, k, 2])
                parts = stats[:, seqs, :].rearrange("p n (a k) -> p n a k", a=2)
                chain(nc.vector.tensor_tensor(dev[:, seqs], parts[:, :, :, 1], mu2, ALU.subtract))
                chain(nc.vector.tensor_tensor(dev2[:, seqs], dev[:, seqs], dev[:, seqs], ALU.mult))
                nc.vector.scalar_tensor_tensor(out=dev2[:, seqs], in0=parts[:, :, :, 2], scalar=2.0 / S, in1=dev2[:, seqs], op0=ALU.mult,
                                               op1=ALU.add).then_inc(dve_q, 1)
                dve.wait_ge(pe_var, g + 1)
                chain(nc.vector.tensor_reduce(var[:, seqs], ps_m[:, 64:64 + 2 * k].rearrange("p (n a) -> p n a", a=2), X, ALU.add))
                nc.vector.tensor_scalar_add(var[:, seqs], var[:, seqs], EPS).then_inc(dve_var, 1)
                dve.wait_ge(act_root, g + 1)
                chain(nc.vector.reciprocal(y0[:, seqs], root[:, seqs]))
                chain(nc.vector.tensor_tensor(y1[:, seqs], y0[:, seqs], y0[:, seqs], ALU.mult))
                chain(nc.vector.tensor_tensor(y1[:, seqs], y1[:, seqs], var[:, seqs], ALU.mult))
                chain(nc.vector.tensor_scalar(y2[:, seqs], y1[:, seqs], -0.5, 1.5, ALU.mult, ALU.add))
                chain(nc.vector.tensor_tensor(rstd[:, seqs], y0[:, seqs], y2[:, seqs], ALU.mult))
                dve.wait_ge(dma_w, 16 * 6)
                chain(nc.vector.tensor_scalar(xn_scale[:, seqs], rstd[:, seqs], w_sb[:, W_GAMMA:W_GAMMA + 1], None, ALU.mult))
                chain(nc.vector.tensor_tensor(xn_shift[:, seqs], mu[:, seqs], xn_scale[:, seqs], ALU.mult))
                chain(nc.vector.tensor_scalar(xn_shift[:, seqs], xn_shift[:, seqs], -1.0, w_sb[:, W_BETA:W_BETA + 1], ALU.mult, ALU.add))

            def normalise(c):
                need(dve, act_xhi, 2 * (c - 1))
                need(dve, dve_xlo, c - 1)
                for n in range(c * CHUNK, (c + 1) * CHUNK):
                    nc.vector.tensor_scalar(xn[:, c % 2, n % CHUNK, :], x_raw[:, n, :], xn_scale[:, n:n + 1], xn_shift[:, n:n + 1],
                                            ALU.mult, ALU.add).then_inc(dve_xn, 1)

            def x_low(c):
                seqs = slice(c * CHUNK, (c + 1) * CHUNK)
                dve.wait_ge(act_xhi, 2 * c + 1)
                dve.wait_ge(dve_xn, (c + 1) * CHUNK)
                nc.vector.tensor_tensor(x_all[C:P, seqs, 0, :], xn[C:P, c % 2, :, :], x_all[C:P, seqs, 1, :].bitcast(fp32),
                                        ALU.subtract).then_inc(dve_xlo, 1)

            def a_low():
                dve.wait_ge(act_ahi, 2)
                nc.vector.scalar_tensor_tensor(out=a_lo[0:C].rearrange("p h c -> p (h c)"), in0=ps_max[0:C].rearrange("p b s -> p (b s)"),
                                               scalar=C ** -0.5, in1=a_hi[0:C].bitcast(fp32).rearrange("p h c -> p (h c)"), op0=ALU.mult,
                                               op1=ALU.subtract).then_inc(dve_alo, 1)
                row = slice(C + 32, C + 33)
                nc.vector.scalar_tensor_tensor(out=a_lo[row].rearrange("p h c -> p (h c)"), in0=ps_sc[row].rearrange("p b s -> p (b s)"),
                                               scalar=C ** -0.5, in1=a_lo[C:C + 1].bitcast(fp32).rearrange("p h c -> p (h c)"), op0=ALU.mult,
                                               op1=ALU.subtract).then_inc(dve_alo, 1)

            def largest():
                chain(nc.vector.memset(tops[:], 0.0))
                dve.wait_ge(dma_flat, 16)
                nc.vector.tensor_reduce(tops[:, 0:1], ctx_spread, X, ALU.max, apply_absolute_value=True).then_inc(dve_tops, 1)
                dve.wait_ge(act_b, 1)
                nc.vector.tensor_reduce(tops[0:C, 1:2], b_sb[0:C, :], X, ALU.max, apply_absolute_value=True).then_inc(dve_tops, 1)

            def scale_b():
                dve.wait_ge(pe_tops, 1)
                chain(nc.vector.tensor_reduce(top[:], ps_m[0:1, 0:2 * P].rearrange("p (a q) -> p a q", a=2), X, ALU.max))
                nc.vector.tensor_tensor(u_bound[:], top[:, 0:1], top[:, 1:2], ALU.mult).then_inc(dve_bound, 1)
                dve.wait_ge(pe_bound, 1)
                chain(nc.vector.tensor_scalar(u_unscale[:], ps_m[:, S:S + 1], C / U_TOP, 1e-30, ALU.mult, ALU.max))
                chain(nc.vector.reciprocal(u_scale[:], u_unscale[:]))
                chain(nc.vector.tensor_scalar(b_w[0:C, :], b_sb[0:C, :], u_scale[0:C], None, ALU.mult))
                nc.vector.scalar_tensor_tensor(out=b_w[C:P, :], in0=b_sb[0:C, :], scalar=u_scale[0:C], in1=b_w[0:C, :].bitcast(fp32),
                                               op0=ALU.mult, op1=ALU.subtract).then_inc(dve_bw, 1)

            statistics(0, *GROUPS[0])
            normalise(0)
            a_low()
            dve.wait_ge(pe_bw, 1)
            nc.vector.tensor_tensor(bo2[:], ps_z[:, 1, 0:1], w_sb[:, W_BO:W_BO + 1], ALU.add).then_inc(dve_bw, 1)
            x_low(0)

            def step(n, half, par, h):
                if peeled_step(n, h, -1, 0):
                    statistics(1, *GROUPS[1])
                    normalise(1)
                if peeled_step(n, h, -1, 1):
                    x_low(1)
                    largest()
                if peeled_step(n, h, -1, 2):
                    normalise(2)
                if peeled_step(n, h, -1, 3):
                    x_low(2)
                    scale_b()
                if peeled_step(n, h, -1, 4):
                    normalise(3)
                if peeled_step(n, h, -1, 5):
                    x_low(3)
                if h % 2 == 0 and (e := at(n, h, T_AHEAD)):
                    m, dn, head = e
                    q = (par + dn) % 2
                    need(dve, act_thi, m * PAIRS + head // 2 + 1)
                    nc.vector.tensor_tensor(t_a[C:P, q, head:head + 2, :].rearrange("p h s -> p (h s)"),
                                            t_bank(m * PAIRS + head // 2)[C:P, :],
                                            t_a[0:C, q, head:head + 2, :].bitcast(fp32).rearrange("p h s -> p (h s)"),
                                            ALU.subtract).then_inc(dve_tlo, 1)
                z_step = at(n, h, -AV_BEHIND) if h % 2 == 0 else None
                if e := z_step:
                    m, dn, head = e
                    sums = ps_z[:, head // 2 % 2, 0:4 * Z_W].rearrange("p (t k z) -> p t k z", t=KT, k=2)
                    inv = inv_sum[:, head // 2 % 2, :].rearrange("p (t k z) -> p t k z", t=KT, k=2)
                    need(dve, pe_av, m * H + head + 1)
                    nc.vector.reciprocal(inv, sums[:, :, :, C:C + 1]).then_inc(dve_inv, 1)
                if e := at(n, h, MAX_AHEAD):
                    m, dn, head = e
                    need(dve, pe_s1, m * H + head + 1)
                    nc.vector.tensor_reduce(neg_max[:, (par + dn) % 2, head, :],
                                            ps_max[:, head % 2, :].rearrange("p (t s) -> p t s", t=KT), X, ALU.max,
                                            negate=True).then_inc(dve_max, 1)
                if e := z_step:
                    m, dn, head = e
                    need(dve, dve_inv, m * PAIRS + head // 2 + 1)
                    nc.vector.tensor_tensor(z_n[:, (par + dn) % 2, :, head // 2 * P:(head // 2 + 1) * P].rearrange("p t (k c) -> p t k c", k=2),
                                            sums[:, :, :, 0:C], inv.broadcast_to([P, KT, 2, C]), ALU.mult).then_inc(dve_zn, 1)
                if h == 1 and (e := at(n, 0, -2 * H)):
                    m, dn, _ = e
                    q = (par + dn) % 2
                    need(dve, pe_y, m + 1)
                    if isinstance(m, int):
                        need(dve, pool_xb, KT * (N // CHUNK))
                    nc.vector.scalar_tensor_tensor(out=x_res[:, bass.ds(m, 1), :], in0=ps_m[:, 0:P].rearrange("p (o s) -> p o s", o=1),
                                                   scalar=u_unscale[:], in1=x_res[:, bass.ds(m, 1), :], op0=ALU.mult,
                                                   op1=ALU.add).then_inc(dve_y, 1)
                if h in (3, 7) and (e := at(n, 0, H)):
                    m, dn, _ = e
                    q, kt = (par + dn) % 2, h // 4
                    need(dve, act_uhi, 2 * m + kt + 1)
                    nc.vector.tensor_tensor(u_lo[:, q, kt, :, :], ps_m[:].rearrange("p (h c) -> p h c", h=H), u_hi[:, q, kt, :, 0:C],
                                            ALU.subtract).then_inc(dve_ulo, 1)

            run(dve, step)


def kernel(x, ctx_2048, L0_xattn_gamma, L0_xattn_beta, L0_xattn_Wq, L0_xattn_bq, L0_xattn_Wkv, L0_xattn_bkv, L0_xattn_Wo,
           L0_xattn_bo):
    import numpy as np
    import concourse.bacc as bacc
    from concourse.bass_utils import run_bass_kernel_spmd

    def heads(w):
        w = np.asarray(w).reshape(H, C, -1)
        return w.transpose(1, 0, 2).reshape(C, -1)

    wkv, bkv = np.asarray(L0_xattn_Wkv), np.asarray(L0_xattn_bkv)
    packed = np.concatenate(
        [heads(wkv[H * C:]), heads(np.asarray(L0_xattn_Wo).T),
         heads(L0_xattn_bq), heads(bkv[H * C:]), np.asarray(L0_xattn_bo)[:, None], np.asarray(L0_xattn_gamma)[:, None],
         np.asarray(L0_xattn_beta)[:, None]], axis=1)
    ctx = np.asarray(ctx_2048)
    arrays = {
        "x": np.ascontiguousarray(np.asarray(x).transpose(1, 0, 2)),
        "ctx": np.ascontiguousarray(ctx.transpose(1, 0, 2)),
        "ctx_flat": np.ascontiguousarray(ctx.reshape(P, -1)),
        "wq": np.ascontiguousarray(heads(L0_xattn_Wq).reshape(C, H, C)),
        "wk": np.ascontiguousarray(heads(wkv[:H * C]).reshape(C, H, C)),
        "w": np.ascontiguousarray(packed),
    }
    nc = bacc.Bacc("TRN2", target_bir_lowering=False, num_devices=1)
    ins = [nc.dram_tensor(k, a.shape, mybir.dt.float32, kind="ExternalInput").ap() for k, a in arrays.items()]
    out = nc.dram_tensor("out", (P, N, P), mybir.dt.float32, kind="ExternalOutput").ap()
    xattn_program(nc, *ins, out)
    got = run_bass_kernel_spmd(nc, [arrays], core_ids=[0])
    y = np.asarray(got.results[0]["out"]).reshape(KT, C, N, P)
    return np.ascontiguousarray(y.transpose(2, 1, 0, 3)).reshape(N, C, S)
```

```python
import concourse.bass as bass
import concourse.mybir as mybir
from concourse.alu_op_type import AluOpType as ALU
from contextlib import ExitStack

N, C, S, H = 16, 64, 256, 8
P = 128
KT = S // P
PAIRS = H // 2
EPS = 1e-5
DIRECT = 2
T_EARLY = 6
T_AHEAD, MAX_AHEAD, AV_BEHIND = 14, 12, 3
CHUNK = 4
PIECES = ((0, 1), (1, 4), (4, 8), (8, 12), (12, 16))
U_TOP = 16384.0
U_W = C + 2
W_V, W_O, W_BV = 0, H * C, 2 * H * C
W_BO = W_BV + H
W_GAMMA, W_BETA = W_BO + 1, W_BO + 2
W_COLS = W_BETA + 1


def xattn_program(nc, x_in, x_tiles_in, ctx_in, ctx_flat_in, wq_in, wk_in, w_in, out):
    fp32, fp32r, fp16 = mybir.dt.float32, mybir.dt.float32r, mybir.dt.float16
    ACT = mybir.ActivationFunctionType
    X = mybir.AxisListType.X
    stack = ExitStack()
    with stack:
        def sb(name, shape, dt):
            return stack.enter_context(nc.sbuf_tensor(name, shape, dt))

        def ps(name, shape):
            return stack.enter_context(nc.psum_tensor(name, shape, fp32))

        def sem(name):
            return stack.enter_context(nc.semaphore(name))

        x_raw = sb("x_raw", [C, N, S], fp32)
        ctx_raw = sb("ctx_raw", [P, N, S], fp32)
        w_sb = sb("w_sb", [P, W_COLS], fp32)
        xn = sb("xn", [C, 2, CHUNK, S], fp32)
        x_all = sb("x_all", [P, N, 2, S], fp32r)
        c_all = sb("c_all", [P, N, 2, S], fp32r)
        a_hi = sb("a_hi", [P, H, 2 * C], fp32r)
        a_lo = sb("a_lo", [P, H, 2 * C], fp32r)
        b_w = sb("b_w", [P, H * C], fp32r)
        bo2 = sb("bo2", [P, 1], fp32)
        x_res = sb("x_res", [P, N, P], fp32)
        x_seq = sb("x_seq", [P, 2, 2, S], fp32r)
        c_max = sb("c_max", [P, 2, S], fp32r)
        c_seq = sb("c_seq", [P, 2, 2, S], fp32r)
        u_hi = sb("u_hi", [P, 2, KT, H, U_W], fp16)
        u_lo = sb("u_lo", [P, 2, KT, H, C], fp16)
        t_a = sb("t_a", [P, 2, H, S], fp32r)
        t_b = sb("t_b", [P, 2, H, S], fp32r)
        neg_max = sb("neg_max", [P, 2, H, KT], fp32)
        neg_max_rows = sb("neg_max_rows", [H * KT, 2, P], fp32r)
        p_full = sb("p_full", [P, 2, KT * S], fp32)
        b_sb = p_full[:, 0, :]
        wk_sb = p_full[0:C, 1, :].rearrange("p (h c) -> p h c", h=H)
        p_hi = sb("p_hi", [P, 4, KT, S], fp16)
        wq_bq = p_hi[0:C].rearrange("p b t s -> p (b t s)").bitcast(fp32).rearrange("p (h c) -> p h c", h=H)
        p_lo = sb("p_lo", [P, 4, KT, S], fp16)
        inv_sum = sb("inv_sum", [P, 2, 4], fp32)
        z_n = sb("z_n", [P, 2, KT, H * C], fp32)
        ctx_spread = z_n[:].rearrange("p q t k -> p (q t k)")
        z_4 = sb("z_4", [P, KT, 4 * C], fp32)
        z_2 = sb("z_2", [P, KT, 2 * C], fp32)
        z_1 = sb("z_1", [P, KT, C], fp32)
        ident = sb("ident", [P, P], fp32)
        mean_w = sb("mean_w", [P, P], fp32)
        ones_row = sb("ones_row", [1, P], fp32)
        stats = sb("stats", [P, N, 6], fp32)
        dev = sb("dev", [P, N, 2], fp32)
        dev2 = sb("dev2", [P, N, 2], fp32)
        mu = sb("mu", [P, N], fp32)
        var = sb("var", [P, N], fp32)
        root = sb("root", [P, N], fp32)
        y0 = sb("y0", [P, N], fp32)
        y1 = sb("y1", [P, N], fp32)
        y2 = sb("y2", [P, N], fp32)
        rstd = sb("rstd", [P, N], fp32)
        xn_scale = sb("xn_scale", [P, N], fp32)
        xn_shift = sb("xn_shift", [P, N], fp32)
        tops = sb("tops", [P, 2], fp32)
        top = sb("top", [1, 2], fp32)
        warm = sb("warm", [1, 1], fp32)
        u_bound = sb("u_bound", [1, 1], fp32)
        u_unscale = sb("u_unscale", [P, 1], fp32)
        u_scale = sb("u_scale", [P, 1], fp32)

        ps_max = ps("ps_max", [P, 2, KT * S])
        ps_sc = ps("ps_sc", [P, 2, KT * S])
        ps_z = ps("ps_z", [P, 2, 512])
        ps_t = ps("ps_t", [P, 2 * S])
        ps_m = ps("ps_m", [P, 512])
        Z_W = C + 1

        dma_xt = [sem(f"dma_xt{c}") for c in range(N // CHUNK)]
        dma_x = [sem(f"dma_x{g}") for g in range(2)]
        dma_qk, dma_w, dma_flat = sem("dma_qk"), sem("dma_w"), sem("dma_flat")
        dma_c = [sem(f"dma_c{c}") for c in range(N // CHUNK)]
        pool_const, pool_a0, pool_u1, pool_c1 = sem("pool_const"), sem("pool_a0"), sem("pool_u1"), sem("pool_c1")
        pool_xn, dve_ones = sem("pool_xn"), sem("dve_ones")
        pool_c_hi, pool_c_lo, pool_xb = sem("pool_c_hi"), sem("pool_c_lo"), sem("pool_xb")
        dve_step = sem("dve_step")
        dve_stats, dve_q, dve_var, dve_xn, dve_xlo = sem("dve_stats"), sem("dve_q"), sem("dve_var"), sem("dve_xn"), sem("dve_xlo")
        dve_tops, dve_bound, dve_scale, dve_bw, dve_alo = sem("dve_tops"), sem("dve_bound"), sem("dve_scale"), sem("dve_bw"), sem("dve_alo")
        act_table, act_root, act_ahi, act_xhi, act_b = sem("act_table"), sem("act_root"), sem("act_ahi"), sem("act_xhi"), sem("act_b")
        pe_mean, pe_var, pe_a, pe_bw, pe_tops, pe_bound = sem("pe_mean"), sem("pe_var"), sem("pe_a"), sem("pe_bw"), sem("pe_tops"), sem("pe_bound")
        dma_xseq = [sem(f"dma_xseq{b}") for b in range(2)]
        dma_cmax = [sem(f"dma_cmax{b}") for b in range(2)]
        dma_cseq = [sem(f"dma_cseq{b}") for b in range(2)]
        dma_tb = [[sem(f"dma_tb{b}{p}") for p in range(PAIRS)] for b in range(2)]
        dma_negmax = [sem(f"dma_negmax{b}") for b in range(2)]
        dma_out = [sem(f"dma_out{b}") for b in range(2)]
        pe_t, pe_s1, pe_s2, pe_av = sem("pe_t"), sem("pe_s1"), sem("pe_s2"), sem("pe_av")
        pe_u, pe_mt, pe_y = sem("pe_u"), sem("pe_mt"), sem("pe_y")
        act_thi, act_phi, act_p = sem("act_thi"), sem("act_phi"), sem("act_p")
        dve_tlo, dve_max, dve_inv, dve_zn = sem("dve_tlo"), sem("dve_max"), sem("dve_inv"), sem("dve_zn")
        dve_ulo, dve_y = sem("dve_ulo"), sem("dve_y")
        act_uhi, act_mt = sem("act_uhi"), sem("act_mt")
        pool_plo, pool_z4, dve_z2, dve_z1 = sem("pool_plo"), sem("pool_z4"), sem("dve_z2"), sem("dve_z1")

        block = stack.enter_context(nc.Block())

        def need(eng, s, count):
            if not (isinstance(count, int) and count <= 0):
                eng.wait_ge(s, count)

        def at(n, h, shift):
            dn, head = divmod(h + shift, H)
            seq = n + dn
            if isinstance(seq, int) and not 0 <= seq < N:
                return None
            return seq, dn, head

        def peeled_step(n, h, at_n, at_h):
            return isinstance(n, int) and (n, h) == (at_n, at_h)

        def direct(m):
            return isinstance(m, int) and m < DIRECT

        def chunks_by(n, m):
            return N // CHUNK if n == FIRST - 1 else m // CHUNK + 1

        def pieces_by(n, m):
            return len(PIECES) if n == FIRST - 1 else next(p for p, (_, end) in enumerate(PIECES) if m < end) + 1

        def t_banks(turn):
            return 3 if isinstance(turn, int) and turn < T_EARLY else 1

        def t_bank(turn):
            return (ps_t[:], ps_z[:, 0], ps_z[:, 1])[turn % 3 if t_banks(turn) == 3 else 0]

        PREPARE_X = {(-1, 6): 2, (0, 3): 3, (1, 0): 4}
        FIRST, LAST = 2, 11

        def run(eng, step):
            for n in range(-3, FIRST):
                for h in range(H):
                    step(n, n // 2, n % 2, h)
            with eng.Fori(FIRST // 2, (LAST + 1) // 2) as pair:
                for par in range(2):
                    for h in range(H):
                        step(pair * 2 + par, pair, par, h)
            for n in range(LAST + 1, N + 2):
                for h in range(H):
                    step(n, n // 2, n % 2, h)

        def fills(half, par, dn):
            return half + (par + dn) // 2 + 1

        def chunk(c):
            return slice(c * CHUNK, (c + 1) * CHUNK)

        def load_ctx(eng, c):
            for part in range(2):
                eng.dma_start(ctx_raw[part * C:(part + 1) * C, chunk(c)], ctx_in[:, chunk(c), :]).then_inc(dma_c[c], 16)

        @block.sync
        def _(sp):
            for c in range(N // CHUNK):
                sp.dma_start(x_res[:, chunk(c), :], x_tiles_in[:, chunk(c), :]).then_inc(dma_xt[c], 16)
            sp.dma_start(x_raw[:, chunk(0), :], x_in[:, chunk(0), :]).then_inc(dma_x[0], 16)
            load_ctx(sp, 0)
            sp.dma_start(ctx_spread, ctx_flat_in).then_inc(dma_flat, 16)
            load_ctx(sp, 1)
            sp.dma_start(x_raw[:, CHUNK:N, :], x_in[:, CHUNK:N, :]).then_inc(dma_x[1], 16)
            for c in range(2, N // CHUNK):
                load_ctx(sp, c)
            x_from, x_to, c_from = x_all[:].bitcast(fp32), x_seq[:].bitcast(fp32), c_all[:].bitcast(fp32)
            c_to, c_max_to, rows_from = c_seq[:].bitcast(fp32), c_max[:].bitcast(fp32), neg_max_rows[:].bitcast(fp32)
            t_a_from, t_b_to = t_a[:].bitcast(fp32), t_b[:].bitcast(fp32)

            def step(n, half, par, h):
                if h == 3 and (e := at(n, 0, -2 * H)):
                    m, dn, _ = e
                    need(sp, dve_y, m + 1)
                    sp.dma_start(out[:, bass.ds(m, 1), :], x_res[:, bass.ds(m, 1), :]).then_inc(dma_out[par], 16)
                if h == 1 and (e := at(n, 0, H)):
                    m, dn, _ = e
                    q = (par + dn) % 2
                    need(sp, pe_s2, (n - 1) * H + H)
                    if isinstance(n, int):
                        need(sp, pool_c1, N // CHUNK)
                        need(sp, pool_c_lo, chunks_by(n, m))
                    sp.dma_start(c_to[:, q, :, :], c_from[:, bass.ds(m, 1), :, :].rearrange("p o a s -> p (o a) s")).then_inc(dma_cseq[q], 16)
                if h == 5 and (e := at(n, 0, 3 * H)) and not direct(e[0]):
                    m, dn, _ = e
                    q = (par + dn) % 2
                    need(sp, pe_t, (n + 1) * PAIRS + PAIRS)
                    need(sp, pe_s1, (n + 1) * H + H)
                    if isinstance(n, int):
                        need(sp, act_xhi, pieces_by(n, m))
                        need(sp, dve_xlo, pieces_by(n, m))
                        need(sp, pool_c_hi, chunks_by(n, m))
                    sp.dma_start(x_to[:, q, :, :], x_from[:, bass.ds(m, 1), :, :].rearrange("p o a s -> p (o a) s")).then_inc(dma_xseq[q], 16)
                    sp.dma_start(c_max_to[:, q:q + 1, :], c_from[:, bass.ds(m, 1), 0, :]).then_inc(dma_cmax[q], 16)
                if h % 2 == 1 and (e := at(n, h - 1, T_AHEAD)):
                    m, dn, head = e
                    q = (par + dn) % 2
                    need(sp, act_thi, m * PAIRS + head // 2 + 1)
                    sp.dma_start(t_b_to[0:C, q, head:head + 2, :], t_a_from[0:C, q, head:head + 2, :]).then_inc(dma_tb[q][head // 2], 16)
                if h == 6 and (e := at(n, 0, H)):
                    m, dn, _ = e
                    q = (par + dn) % 2
                    need(sp, pe_s2, n * H)
                    need(sp, act_mt, m + 1)
                    sp.dma_start(t_b_to[C:C + 1, q, :, :].rearrange("o h (t s) -> o (h t) s", t=KT),
                                 rows_from[:, q, :]).then_inc(dma_negmax[q], 16)

            run(sp, step)
            for b in range(2):
                sp.wait_ge(dma_out[b], 16 * (N // 2))

        @block.tensor
        def _(pe):
            mm = nc.tensor.matmul
            def products_a(bank):
                for h in range(bank * H // 2, (bank + 1) * H // 2):
                    col = h % (H // 2) * 2 * C
                    last = mm(ps_max[:, bank, col:col + 2 * C].rearrange("p (d c) -> p d c", d=2), wq_bq[:, h, :],
                              wk_sb[:, h:h + 1, :].broadcast_to([C, 2, C]), start=True, stop=True)
                last.then_inc(pe_a, 1)

            pe.wait_ge(dma_qk, 16 * 2)
            products_a(0)
            pe.wait_ge(pool_const, 4)
            pe.wait_ge(dve_stats, N)
            for a in range(2):
                last = mm(ps_m[:, a * N:(a + 1) * N], mean_w[:], stats[:, :, 1 + 3 * a], start=True, stop=True)
            last.then_inc(pe_mean, 1)
            products_a(1)
            pe.wait_ge(dve_q, 1)
            mm(ps_m[:, 64:64 + 2 * N], mean_w[:], dev2[:].rearrange("p n a -> p (n a)"), start=True, stop=True).then_inc(pe_var, 1)
            pe.wait_ge(dma_w, 16 * 2)
            for h in range(H):
                wo_h = w_sb[0:C, W_O + h * C:W_O + (h + 1) * C]
                mm(ps_sc[0:C, 0, h * C:(h + 1) * C], w_sb[0:C, W_V + h * C:W_V + (h + 1) * C], wo_h, start=True, stop=True)
                for half in range(2):
                    last = mm(ps_sc[half * C:(half + 1) * C, 1, 0:1], wo_h, w_sb[0:C, W_BV + h:W_BV + h + 1], start=(h == 0),
                              stop=(h == H - 1))
            last.then_inc(pe_bw, 1)

            def u_bound_everywhere():
                pe.wait_ge(dve_tops, 2)
                nc.tensor.transpose(ps_m[0:1, 0:P], tops[:, 0:1], ident[:])
                nc.tensor.transpose(ps_m[0:1, P:2 * P], tops[:, 1:2], ident[:]).then_inc(pe_tops, 1)
                pe.wait_ge(dve_bound, 1)
                mm(ps_m[:, S:S + 1], ones_row[:], u_bound[:], start=True, stop=True).then_inc(pe_bound, 1)

            def step(n, half, par, h):
                if peeled_step(n, h, -1, 1):
                    u_bound_everywhere()
                if h % 2 == 0 and (e := at(n, h, T_AHEAD)):
                    m, dn, head = e
                    q, turn = (par + dn) % 2, m * PAIRS + head // 2
                    if direct(m):
                        x_m = x_all[:, m]
                        if head == 0:
                            need(pe, act_xhi, m + 1)
                            need(pe, dve_xlo, m + 1)
                            need(pe, dve_ones, 1)
                        if m == 0 and head % (H // 2) == 0:
                            bank = head // (H // 2)
                            need(pe, act_ahi, 3 * (bank + 1))
                            need(pe, dve_alo, 2 * (bank + 1))
                    else:
                        x_m = x_seq[:, q]
                        if head == 0:
                            need(pe, dma_xseq[q], 16 * (fills(half, par, dn) - 1))
                    need(pe, dve_tlo, turn - t_banks(turn) + 1)
                    bank = t_bank(turn)
                    for k in range(2):
                        mm(bank[:, k * S:(k + 1) * S], a_hi[:, head + k, :], x_m[:, 0, :], start=True, stop=False)
                        last = mm(bank[:, k * S:(k + 1) * S], a_lo[:, head + k, :], x_m[:, 1, :], start=False, stop=True)
                    last.then_inc(pe_t, 1)
                if e := at(n, h, MAX_AHEAD):
                    m, dn, head = e
                    q, bank = (par + dn) % 2, head % 2
                    if direct(m):
                        c_m = c_all[:, m, 0, :]
                        need(pe, pool_c_hi, 1)
                    else:
                        c_m = c_max[:, q, :]
                        if head == 0:
                            need(pe, dma_cmax[q], 16 * (fills(half, par, dn) - 1))
                    if head % 2 == 0:
                        need(pe, dve_tlo, m * PAIRS + head // 2 + 1)
                    need(pe, dve_max, m * H + head - 1)
                    for qt in range(KT):
                        last = mm(ps_max[:, bank, qt * S:(qt + 1) * S], t_a[:, q, head, qt * P:(qt + 1) * P], c_m,
                                  start=True, stop=True)
                    last.then_inc(pe_s1, 1)
                if e := at(n, h, 0):
                    m, dn, head = e
                    bank = head % 2
                    if head == 0:
                        need(pe, dma_cseq[par], 16 * fills(half, par, 0))
                        need(pe, dma_negmax[par], 16 * fills(half, par, 0))
                    if isinstance(m, int) and m == 0 and head == 0:
                        need(pe, act_b, 1)
                        need(pe, dve_bw, 1)
                    if head % 2 == 0:
                        need(pe, dma_tb[par][head // 2], 16 * fills(half, par, 0))
                    need(pe, act_p, m * H + head - 1)
                    for kt in range(KT):
                        keys = slice(kt * P, (kt + 1) * P)
                        mm(ps_sc[:, bank, kt * S:(kt + 1) * S], c_seq[:, par, 0, keys], t_a[:, par, head, :], start=True, stop=False)
                        last = mm(ps_sc[:, bank, kt * S:(kt + 1) * S], c_seq[0:C + 1, par, 1, keys], t_b[0:C + 1, par, head, :],
                                  start=False, stop=True)
                    last.then_inc(pe_s2, 1)
                if e := at(n, h, -AV_BEHIND):
                    m, dn, head = e
                    q, bank, buf = (par + dn) % 2, head // 2 % 2, head % 4
                    if head == 0:
                        need(pe, dve_ulo, 2 * (m + 1))
                    if head % 2 == 0:
                        need(pe, dve_zn, m * PAIRS + head // 2 - 1)
                    need(pe, pool_plo, m * H + head + 1)
                    for qt in range(KT):
                        qs = slice(qt * P, (qt + 1) * P)
                        z0 = (qt * 2 + head % 2) * Z_W
                        for kt in range(KT):
                            u_h, u_l = u_hi[:, q, kt, head, 0:Z_W], u_lo[:, q, kt, head, :]
                            mm(ps_z[:, bank, z0:z0 + Z_W], p_hi[:, buf, kt, qs], u_h, start=(kt == 0), stop=False)
                            mm(ps_z[:, bank, z0:z0 + C], p_hi[:, buf, kt, qs], u_l, start=False, stop=False)
                            last = mm(ps_z[:, bank, z0:z0 + Z_W], p_lo[:, buf, kt, qs], u_h, start=False, stop=(kt == KT - 1))
                    last.then_inc(pe_av, 1)
                if h == 1 and (e := at(n, 0, -2 * H)):
                    m, dn, _ = e
                    need(pe, dve_z1, m + 1)
                    if at(n, 0, 0):
                        need(pe, dve_ulo, 2 * (n + 1))
                    nc.tensor.transpose(ps_m[:, 0:P], z_1[:].rearrange("p t c -> p (t c)"), ident[:]).then_inc(pe_y, 1)
                if h in (3, 7) and (e := at(n, 0, H)):
                    m, dn, _ = e
                    q, kt = (par + dn) % 2, h // 4
                    keys = slice(kt * P, (kt + 1) * P)
                    if kt == 0:
                        need(pe, dma_cseq[q], 16 * fills(half, par, dn))
                        if isinstance(m, int) and m == 0:
                            need(pe, dve_bw, 2)
                        need(pe, dve_y, n - 1)
                    else:
                        need(pe, act_mt, n + 2)
                    mm(ps_m[:], c_seq[:, q, 0, keys], b_w[:], start=True, stop=False)
                    mm(ps_m[:], c_seq[0:C, q, 1, keys], b_w[0:C, :], start=False, stop=True).then_inc(pe_u, 1)
                if h == 5 and (e := at(n, 0, H)):
                    m, dn, _ = e
                    need(pe, dve_max, (m + 1) * H)
                    need(pe, dve_ulo, 2 * m + 1)
                    nc.tensor.transpose(ps_m[0:H * KT, 0:P], neg_max[:, (par + dn) % 2, :, :].rearrange("p h t -> p (h t)"),
                                        ident[:]).then_inc(pe_mt, 1)
            run(pe, step)

        @block.scalar
        def _(act):
            act.dma_start(wq_bq, wq_in).then_inc(dma_qk, 16)
            act.dma_start(wk_sb, wk_in).then_inc(dma_qk, 16)
            act.dma_start(w_sb[0:C, :], w_in).then_inc(dma_w, 16)
            act.dma_start(w_sb[C:P, W_BO:W_COLS], w_in[:, W_BO:W_COLS]).then_inc(dma_w, 16)
            act.wait_ge(pool_const, 3)
            nc.scalar.activation(warm[:], ones_row[:, 0:1], ACT.Sqrt).then_inc(act_table, 1)

            def a_high(bank):
                def hi(to, rows):
                    nc.scalar.activation(to[:, bank * H // 2:(bank + 1) * H // 2, :].rearrange("p h c -> p (h c)"), ps_max[rows, bank, :],
                                         ACT.Copy, scale=C ** -0.5).then_inc(act_ahi, 1)
                act.wait_ge(pe_a, bank + 1)
                hi(a_hi[0:C], slice(0, C))
                hi(a_lo[C:C + 1], slice(C, C + 1))
                hi(a_hi[C:P], slice(0, C))

            def x_high(p):
                first, end = PIECES[p]
                if p < 2:
                    act.wait_ge(dve_xn, end)
                else:
                    act.wait_ge(pool_xn, end - CHUNK)
                for n in range(2):
                    last = nc.scalar.activation(x_all[0:C, first:end, n, :], xn[:, p % 2, 0:end - first, :], ACT.Copy)
                last.then_inc(act_xhi, 1)

            act.wait_ge(pool_a0, 1)
            a_high(0)
            act.wait_ge(dve_var, 1)
            nc.scalar.activation(root[:], var[:], ACT.Sqrt).then_inc(act_root, 1)
            a_high(1)
            act.wait_ge(act_table, 1)
            nc.scalar.activation(warm[:], ones_row[:, 0:1], ACT.Exp).then_inc(act_table, 1)
            x_high(0)
            x_high(1)
            act.wait_ge(pe_bw, 1)
            nc.scalar.activation(b_sb[0:C, :], ps_sc[0:C, 0, :], ACT.Copy).then_inc(act_b, 1)

            def step(n, half, par, h):
                if (p := PREPARE_X.get((n, h)) if isinstance(n, int) else None):
                    x_high(p)
                if h % 2 == 0 and (e := at(n, h, T_AHEAD)):
                    m, dn, head = e
                    need(act, pe_t, m * PAIRS + head // 2 + 1)
                    need(act, pe_s2, (m - 2) * H + head + 2)
                    nc.scalar.activation(t_a[0:C, (par + dn) % 2, head:head + 2, :].rearrange("p h s -> p (h s)"),
                                         t_bank(m * PAIRS + head // 2)[0:C, :], ACT.Copy).then_inc(act_thi, 1)
                if e := at(n, h, 0):
                    m, dn, head = e
                    buf = head % 4
                    scores = ps_sc[:, head % 2, :]
                    need(act, pe_s2, m * H + head + 1)
                    need(act, pe_av, m * H + head - 3)
                    nc.scalar.activation(p_hi[:, buf, :, :].rearrange("p t s -> p (t s)"), scores, ACT.Exp).then_inc(act_phi, 1)
                    need(act, pool_plo, m * H + head - 1)
                    nc.scalar.activation(p_full[:, head % 2, :], scores, ACT.Exp).then_inc(act_p, 1)
                if h in (3, 7) and (e := at(n, 0, H)):
                    m, dn, _ = e
                    q, kt = (par + dn) % 2, h // 4
                    need(act, pe_u, 2 * m + kt + 1)
                    need(act, pe_av, (n - 1) * H + H)
                    if isinstance(m, int):
                        need(act, pool_u1, 1)
                    nc.scalar.activation(u_hi[:, q, kt, :, 0:C], ps_m[:].rearrange("p (h c) -> p h c", h=H), ACT.Copy).then_inc(act_uhi, 1)
                if h == 5 and (e := at(n, 0, H)):
                    m, dn, _ = e
                    q = (par + dn) % 2
                    need(act, pe_mt, m + 1)
                    need(act, dma_negmax[q], 16 * (fills(half, par, dn) - 1))
                    nc.scalar.activation(neg_max_rows[:, q, :], ps_m[0:H * KT, 0:P], ACT.Copy).then_inc(act_mt, 1)

            run(act, step)

        @block.gpsimd
        def _(pool):
            nc.gpsimd.memset(ident[:], 0.0).then_inc(pool_const, 1)
            nc.gpsimd.memset(mean_w[:], 1.0 / (2 * P)).then_inc(pool_const, 1)
            nc.gpsimd.memset(ones_row[:], 1.0).then_inc(pool_const, 1)
            pool.wait_ge(pool_const, 3)
            nc.gpsimd.affine_select(out=ident[:], in_=ident[:], compare_op=ALU.not_equal, fill=1.0, base=0,
                                    pattern=[[-1, P]], channel_multiplier=1).then_inc(pool_const, 1)
            pool.wait_ge(pool_const, 4)
            nc.gpsimd.memset(a_lo[C:P].bitcast(fp32), 0.0).then_inc(pool_a0, 1)
            pool.wait_ge(pool_a0, 1)
            nc.gpsimd.memset(u_hi[:, :, :, :, C:U_W], 1.0).then_inc(pool_u1, 1)
            pool.wait_ge(pool_u1, 1)

            def split_ctx(c):
                pool.wait_ge(dma_c[c], 32)
                nc.gpsimd.tensor_scalar(c_all[:, chunk(c), 0, :], ctx_raw[:, chunk(c), :], 1.0, 1.0, ALU.mult, ALU.mult).then_inc(pool_c_hi, 1)
                pool.wait_ge(pool_c_hi, c + 1)
                nc.gpsimd.tensor_tensor(c_all[0:C, chunk(c), 1, :], ctx_raw[0:C, chunk(c), :], c_all[0:C, chunk(c), 0, :].bitcast(fp32),
                                        ALU.subtract).then_inc(pool_c_lo, 1)
                pool.wait_ge(pool_c_lo, c + 1)

            def ones_under_ctx(c):
                nc.gpsimd.memset(c_all[C:P, chunk(c), 1, :].bitcast(fp32), 1.0).then_inc(pool_c1, 1)
                pool.wait_ge(pool_c1, c + 1)

            def normalise(p):
                first, end = PIECES[p]
                pool.wait_ge(dma_x[1], 16)
                pool.wait_ge(dve_scale, 1)
                need(pool, act_xhi, p - 1)
                need(pool, dve_xlo, p - 1)
                for n in range(first, end):
                    nc.gpsimd.tensor_scalar(xn[:, p % 2, n - first, :], x_raw[:, n, :], xn_scale[0:C, n:n + 1], xn_shift[0:C, n:n + 1],
                                            ALU.mult, ALU.add).then_inc(pool_xn, 1)
                pool.wait_ge(pool_xn, end - CHUNK)

            for c in range(N // CHUNK):
                ones_under_ctx(c)
            split_ctx(0)
            for c in range(1, N // CHUNK):
                split_ctx(c)
                if c == 1:
                    normalise(2)
            pool.wait_ge(dve_bw, 1)
            nc.gpsimd.tensor_scalar(x_res[:], x_res[:], 1.0, bo2[:], ALU.mult, ALU.add).then_inc(pool_xb, 1)

            def step(n, half, par, h):
                if peeled_step(n, h, 0, 0):
                    normalise(3)
                if peeled_step(n, h, 0, 4):
                    normalise(4)
                if e := at(n, h, 0):
                    m, dn, head = e
                    buf = head % 4
                    need(pool, act_p, m * H + head + 1)
                    need(pool, pe_av, m * H + head - 3)
                    nc.gpsimd.tensor_tensor(p_lo[:, buf, :, :].rearrange("p t s -> p (t s)"), p_full[:, head % 2, :],
                                            p_hi[:, buf, :, :].rearrange("p t s -> p (t s)"), ALU.subtract).then_inc(pool_plo, 1)
                if h == 3 and (e := at(n, 0, -H)):
                    m, dn, _ = e
                    z = z_n[:, (par + dn) % 2, :, :]
                    need(pool, dve_zn, (m + 1) * PAIRS)
                    need(pool, dve_z2, m)
                    nc.gpsimd.tensor_tensor(z_4[:], z[:, :, 0:4 * C], z[:, :, 4 * C:8 * C], ALU.add).then_inc(pool_z4, 1)

            run(pool, step)

        @block.vector
        def _(dve):
            steps = [0]

            def chain(instruction):
                steps[0] += 1
                instruction.then_inc(dve_step, 1)
                dve.wait_ge(dve_step, steps[0])

            def normalise(p):
                first, end = PIECES[p]
                for n in range(first, end):
                    nc.vector.tensor_scalar(xn[:, p % 2, n - first, :], x_raw[:, n, :], xn_scale[0:C, n:n + 1], xn_shift[0:C, n:n + 1],
                                            ALU.mult, ALU.add).then_inc(dve_xn, 1)

            def x_low(p):
                first, end = PIECES[p]
                dve.wait_ge(act_xhi, p + 1)
                nc.vector.tensor_tensor(x_all[C:P, first:end, 0, :], xn[:, p % 2, 0:end - first, :],
                                        x_all[0:C, first:end, 1, :].bitcast(fp32), ALU.subtract).then_inc(dve_xlo, 1)

            def a_low(bank):
                dve.wait_ge(act_ahi, 3 * bank + 2)
                for to, hi in ((slice(0, C), a_hi[0:C]), (slice(C + 32, C + 33), a_lo[C:C + 1])):
                    heads = slice(bank * H // 2, (bank + 1) * H // 2)
                    nc.vector.scalar_tensor_tensor(out=a_lo[to, heads, :].rearrange("p h c -> p (h c)"), in0=ps_max[to, bank, :],
                                                   scalar=C ** -0.5, in1=hi[:, heads, :].bitcast(fp32).rearrange("p h c -> p (h c)"),
                                                   op0=ALU.mult, op1=ALU.subtract).then_inc(dve_alo, 1)

            def largest():
                chain(nc.vector.memset(tops[:], 0.0))
                dve.wait_ge(dma_flat, 16)
                nc.vector.tensor_reduce(tops[:, 0:1], ctx_spread, X, ALU.max, apply_absolute_value=True).then_inc(dve_tops, 1)
                dve.wait_ge(act_b, 1)
                nc.vector.tensor_reduce(tops[0:C, 1:2], b_sb[0:C, :], X, ALU.max, apply_absolute_value=True).then_inc(dve_tops, 1)

            def scale_b():
                dve.wait_ge(pe_tops, 1)
                chain(nc.vector.tensor_reduce(top[:], ps_m[0:1, 0:2 * P].rearrange("p (a q) -> p a q", a=2), X, ALU.max))
                nc.vector.tensor_tensor(u_bound[:], top[:, 0:1], top[:, 1:2], ALU.mult).then_inc(dve_bound, 1)
                dve.wait_ge(pe_bound, 1)
                chain(nc.vector.tensor_scalar(u_unscale[:], ps_m[:, S:S + 1], C / U_TOP, 1e-30, ALU.mult, ALU.max))
                chain(nc.vector.reciprocal(u_scale[:], u_unscale[:]))
                chain(nc.vector.tensor_scalar(b_w[0:C, :], b_sb[0:C, :], u_scale[0:C], None, ALU.mult))
                nc.vector.scalar_tensor_tensor(out=b_w[C:P, :], in0=b_sb[0:C, :], scalar=u_scale[0:C], in1=b_w[0:C, :].bitcast(fp32),
                                               op0=ALU.mult, op1=ALU.subtract).then_inc(dve_bw, 1)

            nc.vector.memset(x_all[C:P, :, 1, :].bitcast(fp32), 1.0).then_inc(dve_ones, 1)
            for n in range(N):
                if n % CHUNK == 0:
                    dve.wait_ge(dma_xt[n // CHUNK], 16)
                nc.vector.bn_stats(stats[:, n, :], x_res[:, n, :]).then_inc(dve_stats, 1)
            dve.wait_ge(pe_mean, 1)
            chain(nc.vector.tensor_reduce(mu[:], ps_m[:, 0:2 * N].rearrange("p (a n) -> p n a", a=2), X, ALU.add))
            mu2 = mu[:].rearrange("p (n a) -> p n a", a=1).broadcast_to([P, N, 2])
            parts = stats[:].rearrange("p n (a k) -> p n a k", a=2)
            chain(nc.vector.tensor_tensor(dev[:], parts[:, :, :, 1], mu2, ALU.subtract))
            chain(nc.vector.tensor_tensor(dev2[:], dev[:], dev[:], ALU.mult))
            nc.vector.scalar_tensor_tensor(out=dev2[:], in0=parts[:, :, :, 2], scalar=2.0 / P, in1=dev2[:], op0=ALU.mult,
                                           op1=ALU.add).then_inc(dve_q, 1)
            dve.wait_ge(pe_var, 1)
            chain(nc.vector.tensor_reduce(var[:], ps_m[:, 64:64 + 2 * N].rearrange("p (n a) -> p n a", a=2), X, ALU.add))
            nc.vector.tensor_scalar_add(var[:], var[:], EPS).then_inc(dve_var, 1)
            dve.wait_ge(act_root, 1)
            chain(nc.vector.reciprocal(y0[:], root[:]))
            chain(nc.vector.tensor_tensor(y1[:], y0[:], y0[:], ALU.mult))
            chain(nc.vector.tensor_tensor(y1[:], y1[:], var[:], ALU.mult))
            chain(nc.vector.tensor_scalar(y2[:], y1[:], -0.5, 1.5, ALU.mult, ALU.add))
            chain(nc.vector.tensor_tensor(rstd[:], y0[:], y2[:], ALU.mult))
            dve.wait_ge(dma_w, 16 * 2)
            chain(nc.vector.tensor_scalar(xn_scale[0:C], rstd[0:C], w_sb[0:C, W_GAMMA:W_GAMMA + 1], None, ALU.mult))
            chain(nc.vector.tensor_tensor(xn_shift[0:C], mu[0:C], xn_scale[0:C], ALU.mult))
            nc.vector.tensor_scalar(xn_shift[0:C], xn_shift[0:C], -1.0, w_sb[0:C, W_BETA:W_BETA + 1], ALU.mult, ALU.add).then_inc(dve_scale, 1)
            dve.wait_ge(dve_scale, 1)
            dve.wait_ge(dma_x[0], 16)
            normalise(0)
            normalise(1)
            a_low(0)
            x_low(0)
            a_low(1)
            x_low(1)
            dve.wait_ge(pe_bw, 1)
            nc.vector.tensor_tensor(bo2[:], ps_sc[:, 1, 0:1], w_sb[:, W_BO:W_BO + 1], ALU.add).then_inc(dve_bw, 1)

            def step(n, half, par, h):
                if peeled_step(n, h, -2, 5):
                    largest()
                if peeled_step(n, h, -1, 1):
                    scale_b()
                if (p := PREPARE_X.get((n, h)) if isinstance(n, int) else None):
                    x_low(p)
                if h % 2 == 0 and (e := at(n, h, T_AHEAD)):
                    m, dn, head = e
                    q = (par + dn) % 2
                    need(dve, act_thi, m * PAIRS + head // 2 + 1)
                    nc.vector.tensor_tensor(t_a[C:P, q, head:head + 2, :].rearrange("p h s -> p (h s)"),
                                            t_bank(m * PAIRS + head // 2)[C:P, :],
                                            t_a[0:C, q, head:head + 2, :].bitcast(fp32).rearrange("p h s -> p (h s)"),
                                            ALU.subtract).then_inc(dve_tlo, 1)
                z_step = at(n, h, -AV_BEHIND) if h % 2 == 0 else None
                if e := z_step:
                    m, dn, head = e
                    sums = ps_z[:, head // 2 % 2, 0:4 * Z_W].rearrange("p (t k z) -> p t k z", t=KT, k=2)
                    inv = inv_sum[:, head // 2 % 2, :].rearrange("p (t k z) -> p t k z", t=KT, k=2)
                    need(dve, pe_av, m * H + head + 1)
                    nc.vector.reciprocal(inv, sums[:, :, :, C:C + 1]).then_inc(dve_inv, 1)
                if e := at(n, h, MAX_AHEAD):
                    m, dn, head = e
                    need(dve, pe_s1, m * H + head + 1)
                    nc.vector.tensor_reduce(neg_max[:, (par + dn) % 2, head, :],
                                            ps_max[:, head % 2, :].rearrange("p (t s) -> p t s", t=KT), X, ALU.max,
                                            negate=True).then_inc(dve_max, 1)
                if e := z_step:
                    m, dn, head = e
                    need(dve, dve_inv, m * PAIRS + head // 2 + 1)
                    nc.vector.tensor_tensor(z_n[:, (par + dn) % 2, :, head // 2 * P:(head // 2 + 1) * P].rearrange("p t (k c) -> p t k c", k=2),
                                            sums[:, :, :, 0:C], inv.broadcast_to([P, KT, 2, C]), ALU.mult).then_inc(dve_zn, 1)
                if h == 5 and (e := at(n, 0, -H)):
                    m, dn, _ = e
                    need(dve, pool_z4, m + 1)
                    nc.vector.tensor_tensor(z_2[:], z_4[:, :, 0:2 * C], z_4[:, :, 2 * C:4 * C], ALU.add).then_inc(dve_z2, 1)
                if h == 7 and (e := at(n, 0, -H)):
                    m, dn, _ = e
                    need(dve, dve_z2, m + 1)
                    need(dve, pe_y, m)
                    nc.vector.tensor_tensor(z_1[:], z_2[:, :, 0:C], z_2[:, :, C:2 * C], ALU.add).then_inc(dve_z1, 1)
                if h == 1 and (e := at(n, 0, -2 * H)):
                    m, dn, _ = e
                    q = (par + dn) % 2
                    need(dve, pe_y, m + 1)
                    if isinstance(m, int):
                        need(dve, pool_xb, 1)
                    nc.vector.scalar_tensor_tensor(out=x_res[:, bass.ds(m, 1), :], in0=ps_m[:, 0:P].rearrange("p (o s) -> p o s", o=1),
                                                   scalar=u_unscale[:], in1=x_res[:, bass.ds(m, 1), :], op0=ALU.mult,
                                                   op1=ALU.add).then_inc(dve_y, 1)
                if h in (3, 7) and (e := at(n, 0, H)):
                    m, dn, _ = e
                    q, kt = (par + dn) % 2, h // 4
                    need(dve, act_uhi, 2 * m + kt + 1)
                    nc.vector.tensor_tensor(u_lo[:, q, kt, :, :], ps_m[:].rearrange("p (h c) -> p h c", h=H), u_hi[:, q, kt, :, 0:C],
                                            ALU.subtract).then_inc(dve_ulo, 1)

            run(dve, step)


def kernel(x, ctx_2048, L0_xattn_gamma, L0_xattn_beta, L0_xattn_Wq, L0_xattn_bq, L0_xattn_Wkv, L0_xattn_bkv, L0_xattn_Wo,
           L0_xattn_bo):
    import numpy as np
    import concourse.bacc as bacc
    from concourse.bass_utils import run_bass_kernel_spmd

    def heads(w):
        w = np.asarray(w).reshape(H, C, -1)
        return w.transpose(1, 0, 2).reshape(C, -1)

    wkv, bkv = np.asarray(L0_xattn_Wkv), np.asarray(L0_xattn_bkv)
    packed = np.concatenate(
        [heads(wkv[H * C:]), heads(np.asarray(L0_xattn_Wo).T),
         heads(bkv[H * C:]), np.asarray(L0_xattn_bo)[:, None], np.asarray(L0_xattn_gamma)[:, None],
         np.asarray(L0_xattn_beta)[:, None]], axis=1)
    x, ctx = np.asarray(x), np.asarray(ctx_2048)
    bq = heads(L0_xattn_bq).reshape(C, H, 1)
    wq_bq = np.concatenate([heads(L0_xattn_Wq).reshape(C, H, C), np.broadcast_to(bq, (C, H, C))], axis=2)
    arrays = {
        "x": np.ascontiguousarray(x.transpose(1, 0, 2)),
        "x_tiles": np.ascontiguousarray(x.reshape(N, C, KT, P).transpose(2, 1, 0, 3).reshape(P, N, P)),
        "ctx": np.ascontiguousarray(ctx.transpose(1, 0, 2)),
        "ctx_flat": np.ascontiguousarray(ctx.reshape(P, -1)),
        "wq": np.ascontiguousarray(wq_bq),
        "wk": np.ascontiguousarray(heads(wkv[:H * C]).reshape(C, H, C)),
        "w": np.ascontiguousarray(packed),
    }
    nc = bacc.Bacc("TRN2", target_bir_lowering=False, num_devices=1)
    ins = [nc.dram_tensor(k, a.shape, mybir.dt.float32, kind="ExternalInput").ap() for k, a in arrays.items()]
    out = nc.dram_tensor("out", (P, N, P), mybir.dt.float32, kind="ExternalOutput").ap()
    xattn_program(nc, *ins, out)
    got = run_bass_kernel_spmd(nc, [arrays], core_ids=[0])
    y = np.asarray(got.results[0]["out"]).reshape(KT, C, N, P)
    return np.ascontiguousarray(y.transpose(2, 1, 0, 3)).reshape(N, C, S)
```

```python
import concourse.bass as bass
import concourse.mybir as mybir
from concourse.alu_op_type import AluOpType as ALU
from contextlib import ExitStack

N, C, S, H = 16, 64, 256, 8
P = 128
KT = S // P
PAIRS = H // 2
EPS = 1e-5
DIRECT = 2
LO_ON_VECTOR = tuple(range(N * H - 11, N * H, 2))
T_EARLY = 6
T_AHEAD, MAX_AHEAD, AV_BEHIND = 14, 12, 3
CHUNK = 4
PIECES = ((0, 1), (1, 2)) + tuple((n, n + 2) for n in range(2, N, 2))
U_TOP = 16384.0
U_W = C + 2
W_V, W_O, W_BV = 0, H * C, 2 * H * C
W_BO = W_BV + H
W_GAMMA, W_BETA = W_BO + 1, W_BO + 2
W_COLS = W_BETA + 1


def xattn_program(nc, x_in, x_tiles_in, ctx_in, ctx_flat_in, wq_in, wk_in, w_in, out):
    fp32, fp32r, fp16 = mybir.dt.float32, mybir.dt.float32r, mybir.dt.float16
    ACT = mybir.ActivationFunctionType
    X = mybir.AxisListType.X
    stack = ExitStack()
    with stack:
        def sb(name, shape, dt):
            return stack.enter_context(nc.sbuf_tensor(name, shape, dt))

        def ps(name, shape):
            return stack.enter_context(nc.psum_tensor(name, shape, fp32))

        def sem(name):
            return stack.enter_context(nc.semaphore(name))

        x_raw = sb("x_raw", [C, N, S], fp32)
        ctx_raw = sb("ctx_raw", [P, N, S], fp32)
        w_sb = sb("w_sb", [P, W_COLS], fp32)
        xn = sb("xn", [C, N, S], fp32)
        x_all = sb("x_all", [P, N, S], fp32r)
        c_all = sb("c_all", [P, N, S], fp32r)
        a_hi = sb("a_hi", [P, H, 2 * C], fp32r)
        a_lo = sb("a_lo", [P, H, 2 * C], fp32r)
        b_w = sb("b_w", [P, 2, H * C], fp32r)
        bo2 = sb("bo2", [P, 1], fp32)
        x_res = sb("x_res", [P, N, P], fp32)
        x_seq = sb("x_seq", [P, 2, 2, S], fp32r)
        c_max = sb("c_max", [P, 2, S], fp32r)
        c_seq = sb("c_seq", [P, 2, 2, S], fp32r)
        u_hi = sb("u_hi", [P, 2, KT, H, U_W], fp16)
        u_lo = sb("u_lo", [P, 2, KT, H, C], fp16)
        t_a = sb("t_a", [P, 2, H, S], fp32r)
        t_b = sb("t_b", [P, 2, H, S], fp32r)
        neg_max = sb("neg_max", [P, 2, H, KT], fp32)
        neg_max_rows = sb("neg_max_rows", [H * KT, 2, P], fp32r)
        p_full = sb("p_full", [P, 2, KT * S], fp32)
        b_sb = p_full[:, 0, :]
        wk_sb = p_full[0:C, 1, :].rearrange("p (h c) -> p h c", h=H)
        p_hi = sb("p_hi", [P, 4, KT, S], fp16)
        wq_bq = p_hi[0:C].rearrange("p b t s -> p (b t s)").bitcast(fp32).rearrange("p (h c) -> p h c", h=H)
        p_lo = sb("p_lo", [P, 4, KT, S], fp16)
        inv_sum = sb("inv_sum", [P, 2, 4], fp32)
        z_n = sb("z_n", [P, 2, KT, H * C], fp32)
        ctx_spread = z_n[:].rearrange("p q t k -> p (q t k)")
        z_4 = sb("z_4", [P, KT, 4 * C], fp32)
        z_2 = sb("z_2", [P, KT, 2 * C], fp32)
        z_1 = sb("z_1", [P, KT, C], fp32)
        ident = sb("ident", [P, P], fp32)
        mean_w = sb("mean_w", [P, P], fp32)
        ones_row = sb("ones_row", [1, P], fp32)
        stats = sb("stats", [P, N, 6], fp32)
        dev = sb("dev", [P, N, 2], fp32)
        dev2 = sb("dev2", [P, N, 2], fp32)
        mu = sb("mu", [P, N], fp32)
        var = sb("var", [P, N], fp32)
        root = sb("root", [P, N], fp32)
        y0 = sb("y0", [P, N], fp32)
        y1 = sb("y1", [P, N], fp32)
        y2 = sb("y2", [P, N], fp32)
        rstd = sb("rstd", [P, N], fp32)
        xn_scale = sb("xn_scale", [P, N], fp32)
        xn_shift = sb("xn_shift", [P, N], fp32)
        tops = sb("tops", [P, 2], fp32)
        top = sb("top", [1, 2], fp32)
        warm = sb("warm", [1, 1], fp32)
        u_bound = sb("u_bound", [1, 1], fp32)
        u_unscale = sb("u_unscale", [P, 1], fp32)
        u_scale = sb("u_scale", [P, 1], fp32)

        ps_max = ps("ps_max", [P, 2, KT * S])
        ps_sc = ps("ps_sc", [P, 2, KT * S])
        ps_z = ps("ps_z", [P, 2, 512])
        ps_t = ps("ps_t", [P, 2 * S])
        ps_m = ps("ps_m", [P, 512])
        Z_W = C + 1

        dma_xt = [sem(f"dma_xt{c}") for c in range(N // CHUNK)]
        dma_x = [sem(f"dma_x{g}") for g in range(2)]
        dma_qk, dma_w, dma_flat = sem("dma_qk"), sem("dma_w"), sem("dma_flat")
        dma_c = [sem(f"dma_c{c}") for c in range(N // CHUNK)]
        pool_const, pool_a0, pool_u1 = sem("pool_const"), sem("pool_a0"), sem("pool_u1")
        dve_plo, dve_z1 = sem("dve_plo"), sem("dve_z1")
        pool_xn, dve_ones = sem("pool_xn"), sem("dve_ones")
        pool_c_hi, pool_c_lo, pool_xb = sem("pool_c_hi"), sem("pool_c_lo"), sem("pool_xb")
        dve_step = sem("dve_step")
        dve_stats, dve_q, dve_var, dve_xn, dve_xlo = sem("dve_stats"), sem("dve_q"), sem("dve_var"), sem("dve_xn"), sem("dve_xlo")
        dve_tops, dve_bound, dve_scale, dve_bo, dve_uscale, pool_b, dve_alo = sem("dve_tops"), sem("dve_bound"), sem("dve_scale"), sem("dve_bo"), sem("dve_uscale"), sem("pool_b"), sem("dve_alo")
        act_table, act_root, act_ahi, act_xhi, act_b = sem("act_table"), sem("act_root"), sem("act_ahi"), sem("act_xhi"), sem("act_b")
        pe_mean, pe_var, pe_a, pe_bw, pe_tops, pe_bound = sem("pe_mean"), sem("pe_var"), sem("pe_a"), sem("pe_bw"), sem("pe_tops"), sem("pe_bound")
        dma_xseq = [sem(f"dma_xseq{b}") for b in range(2)]
        dma_cmax = [sem(f"dma_cmax{b}") for b in range(2)]
        dma_cseq = [sem(f"dma_cseq{b}") for b in range(2)]
        dma_negmax = [sem(f"dma_negmax{b}") for b in range(2)]
        dma_out = [sem(f"dma_out{b}") for b in range(2)]
        pe_t, pe_s1, pe_s2, pe_av = sem("pe_t"), sem("pe_s1"), sem("pe_s2"), sem("pe_av")
        pe_u, pe_mt, pe_y = sem("pe_u"), sem("pe_mt"), sem("pe_y")
        act_thi, act_phi, act_p = sem("act_thi"), sem("act_phi"), sem("act_p")
        dve_tlo, dve_max, dve_inv, dve_zn = sem("dve_tlo"), sem("dve_max"), sem("dve_inv"), sem("dve_zn")
        dve_ulo, dve_y = sem("dve_ulo"), sem("dve_y")
        act_uhi, act_mt = sem("act_uhi"), sem("act_mt")
        pool_plo, pool_z4, dve_z2, pool_z1 = sem("pool_plo"), sem("pool_z4"), sem("dve_z2"), sem("pool_z1")

        block = stack.enter_context(nc.Block())

        def need(eng, s, count):
            if not (isinstance(count, int) and count <= 0):
                eng.wait_ge(s, count)

        def at(n, h, shift):
            dn, head = divmod(h + shift, H)
            seq = n + dn
            if isinstance(seq, int) and not 0 <= seq < N:
                return None
            return seq, dn, head

        def peeled_step(n, h, at_n, at_h):
            return isinstance(n, int) and (n, h) == (at_n, at_h)

        def direct(m):
            return isinstance(m, int) and m < DIRECT

        def chunks_by(n, m):
            return N // CHUNK if n == FIRST - 1 else m // CHUNK + 1

        def pieces_by(n, m):
            return len(PIECES) if n == FIRST - 1 else next(p for p, (_, end) in enumerate(PIECES) if m < end) + 1

        def last_sequence(m):
            return isinstance(m, int) and m == N - 1

        def lo_done(eng, m, head):
            i = m * H + head
            by_vector = sum(j <= i for j in LO_ON_VECTOR) if isinstance(i, int) else 0
            if isinstance(i, int) and i in LO_ON_VECTOR:
                eng.wait_ge(dve_plo, by_vector)
            else:
                need(eng, pool_plo, i + 1 - by_vector)

        def t_banks(turn):
            return 3 if isinstance(turn, int) and turn < T_EARLY else 1

        def t_bank(turn):
            return (ps_t[:], ps_z[:, 0], ps_z[:, 1])[turn % 3 if t_banks(turn) == 3 else 0]

        X_HIGH_AT = {(-2, 7): 2, (-1, 1): 3, (-1, 3): 4, (-1, 6): 5, (-1, 7): 6, (0, 1): 7, (0, 3): 8}
        X_LOW_AT = {(-1, 2): 2, (-1, 7): 3, (0, 1): 4, (0, 3): 5, (0, 5): 6, (1, 1): 7, (1, 3): 8}
        FIRST, LAST = 2, 11

        def run(eng, step):
            for n in range(-3, FIRST):
                for h in range(H):
                    step(n, n // 2, n % 2, h)
            with eng.Fori(FIRST // 2, (LAST + 1) // 2) as pair:
                for par in range(2):
                    for h in range(H):
                        step(pair * 2 + par, pair, par, h)
            for n in range(LAST + 1, N + 2):
                for h in range(H):
                    step(n, n // 2, n % 2, h)

        def u_step(n, h):
            if isinstance(n, int) and (n, h) in ((-1, 7), (0, 1)):
                return 0, -n, n + 1
            if h in (3, 7) and not (isinstance(n, int) and n < 0) and (e := at(n, 0, H)):
                return e[0], 1, h // 4
            return None

        def fills(half, par, dn):
            return half + (par + dn) // 2 + 1

        def chunk(c):
            return slice(c * CHUNK, (c + 1) * CHUNK)

        def load_ctx(eng, c):
            for part in range(2):
                eng.dma_start(ctx_raw[part * C:(part + 1) * C, chunk(c)], ctx_in[:, chunk(c), :]).then_inc(dma_c[c], 16)

        @block.sync
        def _(sp):
            for c in range(N // CHUNK):
                sp.dma_start(x_res[:, chunk(c), :], x_tiles_in[:, chunk(c), :]).then_inc(dma_xt[c], 16)
            sp.dma_start(x_raw[:, chunk(0), :], x_in[:, chunk(0), :]).then_inc(dma_x[0], 16)
            load_ctx(sp, 0)
            sp.dma_start(ctx_spread, ctx_flat_in).then_inc(dma_flat, 16)
            load_ctx(sp, 1)
            sp.dma_start(x_raw[:, CHUNK:N, :], x_in[:, CHUNK:N, :]).then_inc(dma_x[1], 16)
            for c in range(2, N // CHUNK):
                load_ctx(sp, c)
            x_from, x_to, c_from = x_all[:].bitcast(fp32), x_seq[:].bitcast(fp32), c_all[:].bitcast(fp32)
            c_to, c_max_to, rows_from = c_seq[:].bitcast(fp32), c_max[:].bitcast(fp32), neg_max_rows[:].bitcast(fp32)
            t_b_to = t_b[:].bitcast(fp32)

            def step(n, half, par, h):
                if h == 3 and (e := at(n, 0, -2 * H)):
                    m, dn, _ = e
                    need(sp, dve_y, m + 1)
                    sp.dma_start(out[:, bass.ds(m, 1), :], x_res[:, bass.ds(m, 1), :]).then_inc(dma_out[par], 16)
                if h == 1 and (e := at(n, 0, H)):
                    m, dn, _ = e
                    q = (par + dn) % 2
                    need(sp, pe_s2, (n - 1) * H + H)
                    if isinstance(n, int):
                        need(sp, pool_c_lo, chunks_by(n, m))
                    for slot, rows in ((0, P), (1, C)):
                        sp.dma_start(c_to[0:rows, q, slot:slot + 1, :], c_from[0:rows, bass.ds(m, 1), :]).then_inc(dma_cseq[q], 16)
                if h == 5 and (e := at(n, 0, 3 * H)) and not direct(e[0]):
                    m, dn, _ = e
                    q = (par + dn) % 2
                    need(sp, pe_t, (n + 1) * PAIRS + PAIRS)
                    need(sp, pe_s1, (n + 1) * H + H)
                    if isinstance(n, int):
                        need(sp, act_xhi, pieces_by(n, m))
                        need(sp, dve_xlo, pieces_by(n, m))
                        need(sp, pool_c_lo, chunks_by(n, m))
                    for slot, rows in ((0, P), (1, C)):
                        sp.dma_start(x_to[0:rows, q, slot:slot + 1, :], x_from[0:rows, bass.ds(m, 1), :]).then_inc(dma_xseq[q], 16)
                    sp.dma_start(c_max_to[:, q:q + 1, :], c_from[:, bass.ds(m, 1), :]).then_inc(dma_cmax[q], 16)
                if h == 6 and (e := at(n, 0, H)):
                    m, dn, _ = e
                    q = (par + dn) % 2
                    need(sp, act_mt, m + 1)
                    sp.dma_start(t_b_to[C:C + 1, q, :, :].rearrange("o h (t s) -> o (h t) s", t=KT),
                                 rows_from[:, q, :]).then_inc(dma_negmax[q], 16)

            run(sp, step)
            for b in range(2):
                sp.wait_ge(dma_out[b], 16 * (N // 2))

        @block.tensor
        def _(pe):
            mm = nc.tensor.matmul
            def products_a(bank):
                for h in range(bank * H // 2, (bank + 1) * H // 2):
                    col = h % (H // 2) * 2 * C
                    last = mm(ps_max[:, bank, col:col + 2 * C].rearrange("p (d c) -> p d c", d=2), wq_bq[:, h, :],
                              wk_sb[:, h:h + 1, :].broadcast_to([C, 2, C]), start=True, stop=True)
                last.then_inc(pe_a, 1)

            pe.wait_ge(dma_qk, 16 * 2)
            products_a(0)
            products_a(1)
            pe.wait_ge(pool_const, 4)
            pe.wait_ge(dve_stats, N)
            for a in range(2):
                last = mm(ps_m[:, a * N:(a + 1) * N], mean_w[:], stats[:, :, 1 + 3 * a], start=True, stop=True)
            last.then_inc(pe_mean, 1)
            pe.wait_ge(dve_q, 1)
            mm(ps_m[:, 64:64 + 2 * N], mean_w[:], dev2[:].rearrange("p n a -> p (n a)"), start=True, stop=True).then_inc(pe_var, 1)
            pe.wait_ge(dma_w, 16 * 2)
            for h in range(H):
                wo_h = w_sb[0:C, W_O + h * C:W_O + (h + 1) * C]
                for half in range(2):
                    rows = slice(half * C, (half + 1) * C)
                    mm(ps_sc[rows, 0, h * C:(h + 1) * C], w_sb[0:C, W_V + h * C:W_V + (h + 1) * C], wo_h, start=True, stop=True)
                    last = mm(ps_sc[rows, 1, 0:1], wo_h, w_sb[0:C, W_BV + h:W_BV + h + 1], start=(h == 0), stop=(h == H - 1))
            last.then_inc(pe_bw, 1)

            def step(n, half, par, h):
                if peeled_step(n, h, -2, 7):
                    pe.wait_ge(dve_tops, 2)
                    nc.tensor.transpose(ps_m[0:1, 0:P], tops[:, 0:1], ident[:])
                    nc.tensor.transpose(ps_m[0:1, P:2 * P], tops[:, 1:2], ident[:]).then_inc(pe_tops, 1)
                if peeled_step(n, h, -1, 2):
                    pe.wait_ge(dve_bound, 1)
                    mm(ps_m[:, S:S + 1], ones_row[:], u_bound[:], start=True, stop=True).then_inc(pe_bound, 1)
                if h % 2 == 0 and (e := at(n, h, T_AHEAD)):
                    m, dn, head = e
                    q, turn = (par + dn) % 2, m * PAIRS + head // 2
                    if direct(m):
                        if head == 0:
                            need(pe, act_xhi, m + 1)
                            need(pe, dve_xlo, m + 1)
                            need(pe, dve_ones, 1)
                        if m == 0 and head % (H // 2) == 0:
                            bank = head // (H // 2)
                            need(pe, act_ahi, 3 * (bank + 1))
                            need(pe, dve_alo, 2 * (bank + 1))
                    elif head == 0:
                        need(pe, dma_xseq[q], 32 * (fills(half, par, dn) - 1))
                    need(pe, dve_tlo, turn - t_banks(turn) + 1)
                    bank = t_bank(turn)
                    for k in range(2):
                        mm(bank[:, k * S:(k + 1) * S], a_hi[:, head + k, :], x_seq[:, q, 0, :], start=True, stop=False)
                        last = mm(bank[:, k * S:(k + 1) * S], a_lo[:, head + k, :], x_seq[:, q, 1, :], start=False, stop=True)
                    last.then_inc(pe_t, 1)
                if e := at(n, h, 0):
                    m, dn, head = e
                    bank = head % 2
                    if head == 0:
                        need(pe, dma_cseq[par], 32 * fills(half, par, 0))
                        need(pe, dma_negmax[par], 16 * fills(half, par, 0))
                    if isinstance(m, int) and m == 0 and head == 0:
                        need(pe, act_b, 1)
                        need(pe, dve_bo, 1)
                    if head % 2 == 0:
                        need(pe, dve_tlo, m * PAIRS + head // 2 + 1)
                    need(pe, act_p, m * H + head - 1)
                    for kt in range(KT):
                        keys = slice(kt * P, (kt + 1) * P)
                        mm(ps_sc[:, bank, kt * S:(kt + 1) * S], c_seq[:, par, 0, keys], t_a[:, par, head, :], start=True, stop=False)
                        last = mm(ps_sc[:, bank, kt * S:(kt + 1) * S], c_seq[0:C + 1, par, 1, keys], t_b[0:C + 1, par, head, :],
                                  start=False, stop=True)
                    last.then_inc(pe_s2, 1)
                if e := at(n, h, MAX_AHEAD):
                    m, dn, head = e
                    q, bank = (par + dn) % 2, head % 2
                    if direct(m):
                        c_m = c_all[:, m, :]
                        need(pe, pool_c_lo, 1)
                    else:
                        c_m = c_max[:, q, :]
                        if head == 0:
                            need(pe, dma_cmax[q], 16 * (fills(half, par, dn) - 1))
                    if head % 2 == 0:
                        need(pe, act_thi, m * PAIRS + head // 2 + 1)
                    need(pe, dve_max, m * H + head - 1)
                    for qt in range(KT):
                        last = mm(ps_max[:, bank, qt * S:(qt + 1) * S], t_a[:, q, head, qt * P:(qt + 1) * P], c_m,
                                  start=True, stop=True)
                    last.then_inc(pe_s1, 1)
                if e := at(n, h, -AV_BEHIND):
                    m, dn, head = e
                    q, bank, buf = (par + dn) % 2, head // 2 % 2, head % 4
                    if head == 0:
                        need(pe, dve_ulo, 2 * (m + 1))
                    if head % 2 == 0:
                        need(pe, dve_zn, m * PAIRS + head // 2 - 1)
                    lo_done(pe, m, head)
                    for qt in range(KT):
                        qs = slice(qt * P, (qt + 1) * P)
                        z0 = (qt * 2 + head % 2) * Z_W
                        for kt in range(KT):
                            u_h, u_l = u_hi[:, q, kt, head, 0:Z_W], u_lo[:, q, kt, head, :]
                            mm(ps_z[:, bank, z0:z0 + Z_W], p_hi[:, buf, kt, qs], u_h, start=(kt == 0), stop=False)
                            mm(ps_z[:, bank, z0:z0 + C], p_hi[:, buf, kt, qs], u_l, start=False, stop=False)
                            last = mm(ps_z[:, bank, z0:z0 + Z_W], p_lo[:, buf, kt, qs], u_h, start=False, stop=(kt == KT - 1))
                    last.then_inc(pe_av, 1)
                if h == 1 and (e := at(n, 0, -2 * H)):
                    m, dn, _ = e
                    if last_sequence(m):
                        need(pe, dve_z1, 1)
                    else:
                        need(pe, pool_z1, m + 1)
                    if at(n, 0, 0):
                        need(pe, dve_ulo, 2 * (n + 1))
                    nc.tensor.transpose(ps_m[:, 0:P], z_1[:].rearrange("p t c -> p (t c)"), ident[:]).then_inc(pe_y, 1)
                if e := u_step(n, h):
                    m, dn, kt = e
                    q = (par + dn) % 2
                    keys = slice(kt * P, (kt + 1) * P)
                    if isinstance(m, int) and m == 0:
                        if kt == 0:
                            need(pe, dma_cseq[q], 32)
                            need(pe, pool_b, 3)
                            need(pe, act_mt, 1)
                        else:
                            need(pe, dve_ulo, 1)
                    elif kt == 0:
                        need(pe, dma_cseq[q], 32 * fills(half, par, dn))
                        if isinstance(n, int) and n < 2:
                            need(pe, dve_ulo, 2 * m)
                        else:
                            need(pe, dve_y, n - 1)
                    else:
                        need(pe, act_mt, n + 2)
                    mm(ps_m[:], c_seq[:, q, 0, keys], b_w[:, 0, :], start=True, stop=False)
                    mm(ps_m[:], c_seq[0:C, q, 1, keys], b_w[0:C, 1, :], start=False, stop=True).then_inc(pe_u, 1)
                if h == 5 and (e := at(n, 0, H)):
                    m, dn, _ = e
                    need(pe, dve_max, (m + 1) * H)
                    if isinstance(m, int) and m == 0:
                        need(pe, dve_uscale, 1)
                    else:
                        need(pe, dve_ulo, 2 * m + 1)
                    nc.tensor.transpose(ps_m[0:H * KT, 0:P], neg_max[:, (par + dn) % 2, :, :].rearrange("p h t -> p (h t)"),
                                        ident[:]).then_inc(pe_mt, 1)
            run(pe, step)

        @block.scalar
        def _(act):
            act.dma_start(wq_bq, wq_in).then_inc(dma_qk, 16)
            act.dma_start(wk_sb, wk_in).then_inc(dma_qk, 16)
            act.dma_start(w_sb[0:C, :], w_in).then_inc(dma_w, 16)
            act.dma_start(w_sb[C:P, W_BO:W_COLS], w_in[:, W_BO:W_COLS]).then_inc(dma_w, 16)
            act.wait_ge(pool_const, 3)
            nc.scalar.activation(warm[:], ones_row[:, 0:1], ACT.Sqrt).then_inc(act_table, 1)

            def a_high(bank):
                def hi(to, rows):
                    nc.scalar.activation(to[:, bank * H // 2:(bank + 1) * H // 2, :].rearrange("p h c -> p (h c)"), ps_max[rows, bank, :],
                                         ACT.Copy, scale=C ** -0.5).then_inc(act_ahi, 1)
                act.wait_ge(pe_a, bank + 1)
                hi(a_hi[0:C], slice(0, C))
                hi(a_lo[C:C + 1], slice(C, C + 1))
                hi(a_hi[C:P], slice(0, C))

            def x_high(p):
                first, end = PIECES[p]
                piece = xn[:, first:end, :]
                if first < DIRECT:
                    act.wait_ge(dve_xn, end)
                else:
                    act.wait_ge(pool_xn, end - DIRECT)
                if first < DIRECT:
                    for slot in range(2):
                        last = nc.scalar.activation(x_seq[0:C, first:end, slot, :], piece, ACT.Copy)
                else:
                    last = nc.scalar.activation(x_all[0:C, first:end, :], piece, ACT.Copy)
                last.then_inc(act_xhi, 1)

            act.wait_ge(pool_a0, 1)
            a_high(0)
            a_high(1)
            act.wait_ge(dve_var, 1)
            nc.scalar.activation(root[:], var[:], ACT.Sqrt).then_inc(act_root, 1)
            act.wait_ge(act_table, 1)
            nc.scalar.activation(warm[:], ones_row[:, 0:1], ACT.Exp).then_inc(act_table, 1)
            x_high(0)
            x_high(1)
            act.wait_ge(pe_bw, 1)
            nc.scalar.activation(b_sb, ps_sc[:, 0, :], ACT.Copy).then_inc(act_b, 1)

            def step(n, half, par, h):
                if h % 2 == 0 and (e := at(n, h, T_AHEAD)):
                    m, dn, head = e
                    need(act, pe_t, m * PAIRS + head // 2 + 1)
                    need(act, pe_s2, (m - 2) * H + head + 2)
                    nc.scalar.activation(t_a[:, (par + dn) % 2, head:head + 2, :].rearrange("p h s -> p (h s)"),
                                         t_bank(m * PAIRS + head // 2), ACT.Copy).then_inc(act_thi, 1)
                if e := at(n, h, 0):
                    m, dn, head = e
                    buf = head % 4
                    scores = ps_sc[:, head % 2, :]
                    need(act, pe_s2, m * H + head + 1)
                    need(act, pe_av, m * H + head - 3)
                    nc.scalar.activation(p_hi[:, buf, :, :].rearrange("p t s -> p (t s)"), scores, ACT.Exp).then_inc(act_phi, 1)
                    lo_done(act, m, head - 2)
                    nc.scalar.activation(p_full[:, head % 2, :], scores, ACT.Exp).then_inc(act_p, 1)
                if e := u_step(n, h):
                    m, dn, kt = e
                    q = (par + dn) % 2
                    need(act, pe_u, 2 * m + kt + 1)
                    need(act, pe_av, (m - 1) * H)
                    if isinstance(m, int):
                        need(act, pool_u1, 1)
                    nc.scalar.activation(u_hi[:, q, kt, :, 0:C], ps_m[:].rearrange("p (h c) -> p h c", h=H), ACT.Copy).then_inc(act_uhi, 1)
                if h == 5 and (e := at(n, 0, H)):
                    m, dn, _ = e
                    q = (par + dn) % 2
                    need(act, pe_mt, m + 1)
                    need(act, dma_negmax[q], 16 * (fills(half, par, dn) - 1))
                    nc.scalar.activation(neg_max_rows[:, q, :], ps_m[0:H * KT, 0:P], ACT.Copy).then_inc(act_mt, 1)

                if (p := X_HIGH_AT.get((n, h)) if isinstance(n, int) else None):
                    x_high(p)

            run(act, step)

        @block.gpsimd
        def _(pool):
            nc.gpsimd.memset(ident[:], 0.0).then_inc(pool_const, 1)
            nc.gpsimd.memset(mean_w[:], 1.0 / (2 * P)).then_inc(pool_const, 1)
            nc.gpsimd.memset(ones_row[:], 1.0).then_inc(pool_const, 1)
            pool.wait_ge(pool_const, 3)
            nc.gpsimd.affine_select(out=ident[:], in_=ident[:], compare_op=ALU.not_equal, fill=1.0, base=0,
                                    pattern=[[-1, P]], channel_multiplier=1).then_inc(pool_const, 1)
            pool.wait_ge(pool_const, 4)
            nc.gpsimd.memset(a_lo[C:P].bitcast(fp32), 0.0).then_inc(pool_a0, 1)
            pool.wait_ge(pool_a0, 1)
            nc.gpsimd.memset(u_hi[:, :, :, :, C:U_W], 1.0).then_inc(pool_u1, 1)
            pool.wait_ge(pool_u1, 1)

            def split_ctx(c):
                pool.wait_ge(dma_c[c], 32)
                nc.gpsimd.tensor_scalar(c_all[:, chunk(c), :], ctx_raw[:, chunk(c), :], 1.0, 1.0, ALU.mult, ALU.mult).then_inc(pool_c_hi, 1)
                pool.wait_ge(pool_c_hi, c + 1)
                nc.gpsimd.tensor_tensor(c_all[C:P, chunk(c), :], ctx_raw[C:P, chunk(c), :], c_all[C:P, chunk(c), :].bitcast(fp32),
                                        ALU.subtract).then_inc(pool_c_lo, 1)
                pool.wait_ge(pool_c_lo, c + 1)

            split_ctx(0)
            split_ctx(1)
            for c, seqs in ((0, range(DIRECT, CHUNK)), (1, range(CHUNK, N))):
                pool.wait_ge(dma_x[c], 16)
                pool.wait_ge(dve_scale, 1)
                for n in seqs:
                    nc.gpsimd.tensor_scalar(xn[:, n, :], x_raw[:, n, :], xn_scale[0:C, n:n + 1], xn_shift[0:C, n:n + 1],
                                            ALU.mult, ALU.add).then_inc(pool_xn, 1)
            pool.wait_ge(pool_xn, N - DIRECT)
            split_ctx(2)
            pool.wait_ge(dve_uscale, 1)
            nc.gpsimd.tensor_scalar(b_sb, b_sb, 1.0, u_scale[:], ALU.mult, ALU.mult).then_inc(pool_b, 1)
            pool.wait_ge(pool_b, 1)
            nc.gpsimd.tensor_scalar(b_w[:, 0, :], b_sb, 1.0, 1.0, ALU.mult, ALU.mult).then_inc(pool_b, 1)
            pool.wait_ge(pool_b, 2)
            nc.gpsimd.tensor_tensor(b_w[0:C, 1, :], b_sb[0:C], b_w[0:C, 0, :].bitcast(fp32), ALU.subtract).then_inc(pool_b, 1)
            pool.wait_ge(pool_b, 3)
            split_ctx(3)

            def step(n, half, par, h):
                if peeled_step(n, h, 1, 6):
                    pool.wait_ge(dve_bo, 1)
                    nc.gpsimd.tensor_scalar(x_res[:], x_res[:], 1.0, bo2[:], ALU.mult, ALU.add).then_inc(pool_xb, 1)
                if (e := at(n, h, 0)) and not (isinstance(e[0], int) and e[0] * H + e[2] in LO_ON_VECTOR):
                    m, dn, head = e
                    buf = head % 4
                    need(pool, act_p, m * H + head + 1)
                    need(pool, pe_av, m * H + head - 3)
                    nc.gpsimd.tensor_tensor(p_lo[:, buf, :, :].rearrange("p t s -> p (t s)"), p_full[:, head % 2, :],
                                            p_hi[:, buf, :, :].rearrange("p t s -> p (t s)"), ALU.subtract).then_inc(pool_plo, 1)
                if h == 3 and (e := at(n, 0, -H)) and not last_sequence(e[0]):
                    m, dn, _ = e
                    z = z_n[:, (par + dn) % 2, :, :]
                    need(pool, dve_zn, (m + 1) * PAIRS)
                    need(pool, dve_z2, m)
                    nc.gpsimd.tensor_tensor(z_4[:], z[:, :, 0:4 * C], z[:, :, 4 * C:8 * C], ALU.add).then_inc(pool_z4, 1)

                if h == 6 and (e := at(n, 0, -H)) and not last_sequence(e[0]):
                    m, dn, _ = e
                    need(pool, dve_z2, m + 1)
                    need(pool, pe_y, m)
                    nc.gpsimd.tensor_tensor(z_1[:], z_2[:, :, 0:C], z_2[:, :, C:2 * C], ALU.add).then_inc(pool_z1, 1)

            run(pool, step)

        @block.vector
        def _(dve):
            steps = [0]

            def chain(instruction):
                steps[0] += 1
                instruction.then_inc(dve_step, 1)
                dve.wait_ge(dve_step, steps[0])

            def normalise(p):
                first, end = PIECES[p]
                for n in range(first, end):
                    nc.vector.tensor_scalar(xn[:, n, :], x_raw[:, n, :], xn_scale[0:C, n:n + 1], xn_shift[0:C, n:n + 1],
                                            ALU.mult, ALU.add).then_inc(dve_xn, 1)

            def x_low(p):
                first, end = PIECES[p]
                dve.wait_ge(act_xhi, p + 1)
                to = x_seq[:, first:end, 0, :] if first < DIRECT else x_all[:, first:end, :]
                nc.vector.tensor_tensor(to[C:P], xn[:, first:end, :], to[0:C].bitcast(fp32), ALU.subtract).then_inc(dve_xlo, 1)

            def a_low(bank):
                dve.wait_ge(act_ahi, 3 * (bank + 1))
                for to, hi in ((slice(0, C), a_hi[0:C]), (slice(C + 32, C + 33), a_lo[C:C + 1])):
                    heads = slice(bank * H // 2, (bank + 1) * H // 2)
                    nc.vector.scalar_tensor_tensor(out=a_lo[to, heads, :].rearrange("p h c -> p (h c)"), in0=ps_max[to, bank, :],
                                                   scalar=C ** -0.5, in1=hi[:, heads, :].bitcast(fp32).rearrange("p h c -> p (h c)"),
                                                   op0=ALU.mult, op1=ALU.subtract).then_inc(dve_alo, 1)

            nc.vector.memset(x_seq[C:P, :, 1, :].bitcast(fp32), 1.0).then_inc(dve_ones, 1)
            nc.vector.memset(c_seq[C:P, :, 1, :].bitcast(fp32), 1.0).then_inc(dve_ones, 1)
            for n in range(N):
                if n % CHUNK == 0:
                    dve.wait_ge(dma_xt[n // CHUNK], 16)
                nc.vector.bn_stats(stats[:, n, :], x_res[:, n, :]).then_inc(dve_stats, 1)
            a_low(0)
            dve.wait_ge(pe_mean, 1)
            chain(nc.vector.tensor_reduce(mu[:], ps_m[:, 0:2 * N].rearrange("p (a n) -> p n a", a=2), X, ALU.add))
            mu2 = mu[:].rearrange("p (n a) -> p n a", a=1).broadcast_to([P, N, 2])
            parts = stats[:].rearrange("p n (a k) -> p n a k", a=2)
            chain(nc.vector.tensor_tensor(dev[:], parts[:, :, :, 1], mu2, ALU.subtract))
            chain(nc.vector.tensor_tensor(dev2[:], dev[:], dev[:], ALU.mult))
            nc.vector.scalar_tensor_tensor(out=dev2[:], in0=parts[:, :, :, 2], scalar=2.0 / P, in1=dev2[:], op0=ALU.mult,
                                           op1=ALU.add).then_inc(dve_q, 1)
            a_low(1)
            dve.wait_ge(pe_var, 1)
            chain(nc.vector.tensor_reduce(var[:], ps_m[:, 64:64 + 2 * N].rearrange("p (n a) -> p n a", a=2), X, ALU.add))
            nc.vector.tensor_scalar_add(var[:], var[:], EPS).then_inc(dve_var, 1)
            dve.wait_ge(act_root, 1)
            chain(nc.vector.reciprocal(y0[:], root[:]))
            chain(nc.vector.tensor_tensor(y1[:], y0[:], y0[:], ALU.mult))
            chain(nc.vector.tensor_tensor(y1[:], y1[:], var[:], ALU.mult))
            chain(nc.vector.tensor_scalar(y2[:], y1[:], -0.5, 1.5, ALU.mult, ALU.add))
            chain(nc.vector.tensor_tensor(rstd[:], y0[:], y2[:], ALU.mult))
            dve.wait_ge(dma_w, 16 * 2)
            chain(nc.vector.tensor_scalar(xn_scale[0:C], rstd[0:C], w_sb[0:C, W_GAMMA:W_GAMMA + 1], None, ALU.mult))
            chain(nc.vector.tensor_tensor(xn_shift[0:C], mu[0:C], xn_scale[0:C], ALU.mult))
            nc.vector.tensor_scalar(xn_shift[0:C], xn_shift[0:C], -1.0, w_sb[0:C, W_BETA:W_BETA + 1], ALU.mult, ALU.add).then_inc(dve_scale, 1)
            dve.wait_ge(dve_scale, 1)
            dve.wait_ge(dma_x[0], 16)
            normalise(0)
            normalise(1)
            x_low(0)
            x_low(1)
            dve.wait_ge(dma_flat, 16)
            nc.vector.tensor_reduce(tops[:, 0:1], ctx_spread, X, ALU.max, apply_absolute_value=True).then_inc(dve_tops, 1)
            dve.wait_ge(pe_bw, 1)
            nc.vector.tensor_tensor(bo2[:], ps_sc[:, 1, 0:1], w_sb[:, W_BO:W_BO + 1], ALU.add).then_inc(dve_bo, 1)

            def step(n, half, par, h):
                if peeled_step(n, h, -2, 5):
                    dve.wait_ge(act_b, 1)
                    nc.vector.tensor_reduce(tops[:, 1:2], b_sb, X, ALU.max, apply_absolute_value=True).then_inc(dve_tops, 1)
                if peeled_step(n, h, -1, 0):
                    dve.wait_ge(pe_tops, 1)
                    chain(nc.vector.tensor_reduce(top[:], ps_m[0:1, 0:2 * P].rearrange("p (a q) -> p a q", a=2), X, ALU.max))
                    nc.vector.tensor_tensor(u_bound[:], top[:, 0:1], top[:, 1:2], ALU.mult).then_inc(dve_bound, 1)
                if peeled_step(n, h, -1, 3):
                    dve.wait_ge(pe_bound, 1)
                    chain(nc.vector.tensor_scalar(u_unscale[:], ps_m[:, S:S + 1], C / U_TOP, 1e-30, ALU.mult, ALU.max))
                    nc.vector.reciprocal(u_scale[:], u_unscale[:]).then_inc(dve_uscale, 1)
                if h % 2 == 0 and (e := at(n, h, T_AHEAD)):
                    m, dn, head = e
                    q = (par + dn) % 2
                    need(dve, act_thi, m * PAIRS + head // 2 + 1)
                    nc.vector.tensor_tensor(t_b[0:C, q, head:head + 2, :].rearrange("p h s -> p (h s)"),
                                            t_bank(m * PAIRS + head // 2)[0:C, :],
                                            t_a[0:C, q, head:head + 2, :].bitcast(fp32).rearrange("p h s -> p (h s)"),
                                            ALU.subtract).then_inc(dve_tlo, 1)
                z_step = at(n, h, -AV_BEHIND) if h % 2 == 0 else None
                if e := z_step:
                    m, dn, head = e
                    sums = ps_z[:, head // 2 % 2, 0:4 * Z_W].rearrange("p (t k z) -> p t k z", t=KT, k=2)
                    inv = inv_sum[:, head // 2 % 2, :].rearrange("p (t k z) -> p t k z", t=KT, k=2)
                    need(dve, pe_av, m * H + head + 1)
                    nc.vector.reciprocal(inv, sums[:, :, :, C:C + 1]).then_inc(dve_inv, 1)
                if e := at(n, h, MAX_AHEAD):
                    m, dn, head = e
                    need(dve, pe_s1, m * H + head + 1)
                    nc.vector.tensor_reduce(neg_max[:, (par + dn) % 2, head, :],
                                            ps_max[:, head % 2, :].rearrange("p (t s) -> p t s", t=KT), X, ALU.max,
                                            negate=True).then_inc(dve_max, 1)
                if e := z_step:
                    m, dn, head = e
                    need(dve, dve_inv, m * PAIRS + head // 2 + 1)
                    nc.vector.tensor_tensor(z_n[:, (par + dn) % 2, :, head // 2 * P:(head // 2 + 1) * P].rearrange("p t (k c) -> p t k c", k=2),
                                            sums[:, :, :, 0:C], inv.broadcast_to([P, KT, 2, C]), ALU.mult).then_inc(dve_zn, 1)
                if h == 5 and (e := at(n, 0, -H)):
                    m, dn, _ = e
                    if last_sequence(m):
                        z = z_n[:, (par + dn) % 2, :, :]
                        need(dve, dve_zn, (m + 1) * PAIRS)
                        chain(nc.vector.tensor_tensor(z_4[:], z[:, :, 0:4 * C], z[:, :, 4 * C:8 * C], ALU.add))
                    else:
                        need(dve, pool_z4, m + 1)
                    nc.vector.tensor_tensor(z_2[:], z_4[:, :, 0:2 * C], z_4[:, :, 2 * C:4 * C], ALU.add).then_inc(dve_z2, 1)
                    if last_sequence(m):
                        need(dve, dve_z2, m + 1)
                        need(dve, pe_y, m)
                        nc.vector.tensor_tensor(z_1[:], z_2[:, :, 0:C], z_2[:, :, C:2 * C], ALU.add).then_inc(dve_z1, 1)
                if h == 1 and (e := at(n, 0, -2 * H)):
                    m, dn, _ = e
                    q = (par + dn) % 2
                    need(dve, pe_y, m + 1)
                    if isinstance(m, int):
                        need(dve, pool_xb, 1)
                    nc.vector.scalar_tensor_tensor(out=x_res[:, bass.ds(m, 1), :], in0=ps_m[:, 0:P].rearrange("p (o s) -> p o s", o=1),
                                                   scalar=u_unscale[:], in1=x_res[:, bass.ds(m, 1), :], op0=ALU.mult,
                                                   op1=ALU.add).then_inc(dve_y, 1)
                if e := u_step(n, h):
                    m, dn, kt = e
                    q = (par + dn) % 2
                    need(dve, act_uhi, 2 * m + kt + 1)
                    nc.vector.tensor_tensor(u_lo[:, q, kt, :, :], ps_m[:].rearrange("p (h c) -> p h c", h=H), u_hi[:, q, kt, :, 0:C],
                                            ALU.subtract).then_inc(dve_ulo, 1)

                if isinstance(n, int) and n * H + h in LO_ON_VECTOR:
                    dve.wait_ge(act_p, n * H + h + 1)
                    dve.wait_ge(pe_av, n * H + h - 3)
                    nc.vector.tensor_tensor(p_lo[:, h % 4, :, :].rearrange("p t s -> p (t s)"), p_full[:, h % 2, :],
                                            p_hi[:, h % 4, :, :].rearrange("p t s -> p (t s)"), ALU.subtract).then_inc(dve_plo, 1)
                if (p := X_LOW_AT.get((n, h)) if isinstance(n, int) else None):
                    x_low(p)

            run(dve, step)


def kernel(x, ctx_2048, L0_xattn_gamma, L0_xattn_beta, L0_xattn_Wq, L0_xattn_bq, L0_xattn_Wkv, L0_xattn_bkv, L0_xattn_Wo,
           L0_xattn_bo):
    import numpy as np
    import concourse.bacc as bacc
    from concourse.bass_utils import run_bass_kernel_spmd

    def heads(w):
        w = np.asarray(w).reshape(H, C, -1)
        return w.transpose(1, 0, 2).reshape(C, -1)

    wkv, bkv = np.asarray(L0_xattn_Wkv), np.asarray(L0_xattn_bkv)
    packed = np.concatenate(
        [heads(wkv[H * C:]), heads(np.asarray(L0_xattn_Wo).T),
         heads(bkv[H * C:]), np.asarray(L0_xattn_bo)[:, None], np.asarray(L0_xattn_gamma)[:, None],
         np.asarray(L0_xattn_beta)[:, None]], axis=1)
    x, ctx = np.asarray(x), np.asarray(ctx_2048)
    bq = heads(L0_xattn_bq).reshape(C, H, 1)
    wq_bq = np.concatenate([heads(L0_xattn_Wq).reshape(C, H, C), np.broadcast_to(bq, (C, H, C))], axis=2)
    arrays = {
        "x": np.ascontiguousarray(x.transpose(1, 0, 2)),
        "x_tiles": np.ascontiguousarray(x.reshape(N, C, KT, P).transpose(2, 1, 0, 3).reshape(P, N, P)),
        "ctx": np.ascontiguousarray(ctx.transpose(1, 0, 2)),
        "ctx_flat": np.ascontiguousarray(ctx.reshape(P, -1)),
        "wq": np.ascontiguousarray(wq_bq),
        "wk": np.ascontiguousarray(heads(wkv[:H * C]).reshape(C, H, C)),
        "w": np.ascontiguousarray(packed),
    }
    nc = bacc.Bacc("TRN2", target_bir_lowering=False, num_devices=1)
    ins = [nc.dram_tensor(k, a.shape, mybir.dt.float32, kind="ExternalInput").ap() for k, a in arrays.items()]
    out = nc.dram_tensor("out", (P, N, P), mybir.dt.float32, kind="ExternalOutput").ap()
    xattn_program(nc, *ins, out)
    got = run_bass_kernel_spmd(nc, [arrays], core_ids=[0])
    y = np.asarray(got.results[0]["out"]).reshape(KT, C, N, P)
    return np.ascontiguousarray(y.transpose(2, 1, 0, 3)).reshape(N, C, S)
```
